# Optimizing a Trainium2 kernel written in Bass

```python
import numpy as np
import jax
import jax.numpy as jnp

def _softmax(x, axis=-1):
    return jax.nn.softmax(x, axis=axis)

def _gelu(x):
    return jax.nn.gelu(x, approximate=True)

def _silu(x):
    return jax.nn.silu(x)

def _sigmoid(x):
    return jax.nn.sigmoid(x)

def _layernorm(x, axis=-1, eps=1e-05):
    m = jnp.mean(x, axis=axis, keepdims=True)
    v = jnp.var(x, axis=axis, keepdims=True)
    return (x - m) / jnp.sqrt(v + eps)

def _scatter_add(tgt, idx, src, axis=0):
    return tgt.at[idx].add(src)

def _segment_sum(src, seg, n):
    return jax.ops.segment_sum(src, seg, n)
kernel_name = 'mk_gnn_preln_d2_gnn_r8_ed6077'

def setup_inputs(seed: int=0):
    np.random.seed(seed)
    _w = jnp.asarray

    def _rec_inputs():
        import jax
        import jax.numpy as jnp
        _gk = jax.random.key(seed)
        x = -0.0001126 + 1 * jax.random.normal(jax.random.fold_in(_gk, 1), (1250, 768), jnp.float32)
        src = jax.random.randint(jax.random.fold_in(_gk, 2), (20000,), 0, 1250, jnp.int32)
        dst = jnp.minimum((1250 * jax.random.uniform(jax.random.fold_in(_gk, 3), (20000,)) ** 2.0).astype(jnp.int32), 9999)
        _o = jnp.argsort(dst, stable=True)
        src = src[_o]
        dst = dst[_o]
        edge_type_3 = jax.random.randint(jax.random.fold_in(_gk, 12), (20000,), 0, 3, jnp.int32)
        return (x, src, dst, edge_type_3)
    x, src, dst, edge_type_3 = _rec_inputs()

    def _L0_gnn_setup():
        import jax, jax.numpy as jnp
        import numpy as np
        N_NODES = 1250
        key = jax.random.key(seed)
        k1, k2, k3 = jax.random.split(key, 3)
        x = jax.random.normal(k1, (N_NODES, 768), dtype=jnp.float32)
        edge_index = jax.random.randint(k2, (2, 12500), 0, N_NODES, dtype=jnp.int32)
        W = jax.random.normal(k3, (768, 768), dtype=jnp.float32) * (1.0 / np.sqrt(768))
        b = jnp.zeros((768,), dtype=jnp.float32)
        return {'x': x, 'edge_index': edge_index, 'W': W, 'b': b}
    _L0_gnn_all = _L0_gnn_setup()
    _L0_gnn_in = {k: v for k, v in _L0_gnn_all.items() if k in ('W', 'b')}
    del _L0_gnn_all

    def _L1_gnn_setup():
        import jax, jax.numpy as jnp
        import numpy as np
        NEG_SLOPE = 0.2
        EPS = 1e-16
        N_NODES = 4096
        N_EDGES = 20000
        DIM = 768
        HEADS1 = 4
        OUT1 = DIM // HEADS1
        HEADS2 = 1
        OUT2 = DIM
        N_REL = 3

        def rgat_conv(x, W, q, k, b, src, dst, etype, heads, out_ch, n_nodes):
            xr = jnp.einsum('nd,rdf->rnf', x, W)
            oi = xr[etype, dst]
            oj = xr[etype, src]
            qi = oi @ q
            kj = oj @ k
            alpha = jax.nn.leaky_relu(qi + kj, NEG_SLOPE)
            m = jax.ops.segment_max(alpha, dst, num_segments=n_nodes)
            e = jnp.exp(alpha - m[dst])
            z = jax.ops.segment_sum(e, dst, num_segments=n_nodes)
            a = e / (z[dst] + EPS)
            msg = (a[:, :, None] * oj.reshape(-1, heads, out_ch)).reshape(-1, heads * out_ch)
            out = jax.ops.segment_sum(msg, dst, num_segments=n_nodes)
            return out + b
        key = jax.random.key(seed)
        ks = jax.random.split(key, 12)
        s = 0.02
        return {'x': jax.random.normal(ks[0], (N_NODES, DIM), dtype=jnp.float32), 'edge_index': jax.random.randint(ks[1], (2, N_EDGES), 0, N_NODES, dtype=jnp.int64), 'edge_type': jax.random.randint(ks[2], (N_EDGES,), 0, N_REL, dtype=jnp.int64), 'W1': jax.random.normal(ks[3], (N_REL, DIM, HEADS1 * OUT1), dtype=jnp.float32) * s, 'q1': jax.random.normal(ks[4], (HEADS1 * OUT1, HEADS1), dtype=jnp.float32) * s, 'k1': jax.random.normal(ks[5], (HEADS1 * OUT1, HEADS1), dtype=jnp.float32) * s, 'b1': jnp.zeros((HEADS1 * OUT1,), dtype=jnp.float32), 'W2': jax.random.normal(ks[6], (N_REL, DIM, HEADS2 * OUT2), dtype=jnp.float32) * s, 'q2': jax.random.normal(ks[7], (HEADS2 * OUT2, HEADS2), dtype=jnp.float32) * s, 'k2': jax.random.normal(ks[8], (HEADS2 * OUT2, HEADS2), dtype=jnp.float32) * s, 'b2': jnp.zeros((HEADS2 * OUT2,), dtype=jnp.float32)}
    _L1_gnn_all = _L1_gnn_setup()
    _L1_gnn_in = {k: v for k, v in _L1_gnn_all.items() if k in ('W1', 'q1', 'k1', 'b1', 'W2', 'q2', 'k2', 'b2')}
    del _L1_gnn_all
    return {'x': x, 'src': src, 'dst': dst, 'edge_type_3': edge_type_3, 'L0_gnn_W': _L0_gnn_in['W'], 'L0_gnn_b': _L0_gnn_in['b'], 'L1_gnn_W1': _L1_gnn_in['W1'], 'L1_gnn_q1': _L1_gnn_in['q1'], 'L1_gnn_k1': _L1_gnn_in['k1'], 'L1_gnn_b1': _L1_gnn_in['b1'], 'L1_gnn_W2': _L1_gnn_in['W2'], 'L1_gnn_q2': _L1_gnn_in['q2'], 'L1_gnn_k2': _L1_gnn_in['k2'], 'L1_gnn_b2': _L1_gnn_in['b2']}

def reference(x, src, dst, edge_type_3, L0_gnn_W, L0_gnn_b, L1_gnn_W1, L1_gnn_q1, L1_gnn_k1, L1_gnn_b1, L1_gnn_W2, L1_gnn_q2, L1_gnn_k2, L1_gnn_b2):
    import jax
    import jax.numpy as jnp

    def _L0_gnn_ref(x, edge_index, W, b):
        import jax, jax.numpy as jnp
        import numpy as np
        N_NODES = 1250
        n = x.shape[0]
        loops = jnp.arange(n, dtype=edge_index.dtype)
        row = jnp.concatenate([edge_index[0], loops])
        col = jnp.concatenate([edge_index[1], loops])
        ones = jnp.ones(row.shape[0], dtype=x.dtype)
        deg = jax.ops.segment_sum(ones, col, num_segments=n)
        dinv = jnp.where(deg > 0, jax.lax.rsqrt(deg), 0.0)
        norm = dinv[row] * dinv[col]
        h = x @ W
        msg = h[row] * norm[:, None]
        out = jax.ops.segment_sum(msg, col, num_segments=n) + b
        return out

    def _L1_gnn_ref(x, edge_index, edge_type, W1, q1, k1, b1, W2, q2, k2, b2):
        import jax, jax.numpy as jnp
        import numpy as np
        NEG_SLOPE = 0.2
        EPS = 1e-16
        N_NODES = 4096
        N_EDGES = 20000
        DIM = 768
        HEADS1 = 4
        OUT1 = DIM // HEADS1
        HEADS2 = 1
        OUT2 = DIM
        N_REL = 3

        def rgat_conv(x, W, q, k, b, src, dst, etype, heads, out_ch, n_nodes):
            xr = jnp.einsum('nd,rdf->rnf', x, W)
            oi = xr[etype, dst]
            oj = xr[etype, src]
            qi = oi @ q
            kj = oj @ k
            alpha = jax.nn.leaky_relu(qi + kj, NEG_SLOPE)
            m = jax.ops.segment_max(alpha, dst, num_segments=n_nodes)
            e = jnp.exp(alpha - m[dst])
            z = jax.ops.segment_sum(e, dst, num_segments=n_nodes)
            a = e / (z[dst] + EPS)
            msg = (a[:, :, None] * oj.reshape(-1, heads, out_ch)).reshape(-1, heads * out_ch)
            out = jax.ops.segment_sum(msg, dst, num_segments=n_nodes)
            return out + b
        src, dst = (edge_index[0], edge_index[1])
        n = x.shape[0]
        h = rgat_conv(x, W1, q1, k1, b1, src, dst, edge_type, HEADS1, OUT1, n)
        h = jax.nn.elu(h)
        out = rgat_conv(h, W2, q2, k2, b2, src, dst, edge_type, HEADS2, OUT2, n)
        return out
    edge_index = jnp.stack([src, dst])
    h = jnp.maximum(_layernorm(x, axis=-1), 0.0)
    x = x + _L0_gnn_ref(h, edge_index, L0_gnn_W, L0_gnn_b)
    h = jnp.maximum(_layernorm(x, axis=-1), 0.0)
    x = x + _L1_gnn_ref(h, edge_index, edge_type_3, L1_gnn_W1, L1_gnn_q1, L1_gnn_k1, L1_gnn_b1, L1_gnn_W2, L1_gnn_q2, L1_gnn_k2, L1_gnn_b2)
    return x

_drawn_inputs = setup_inputs


def setup_inputs(seed=0):
    import zlib

    import numpy as np

    out = dict(_drawn_inputs(seed))
    spreads = {'L0_gnn_b': (0.0, 0.1), 'L1_gnn_b1': (0.0, 0.278), 'L1_gnn_b2': (0.0, 0.1)}
    factors = {'L1_gnn_q1': 8.0, 'L1_gnn_k1': 8.0, 'L1_gnn_q2': 8.0, 'L1_gnn_k2': 8.0}
    for name, (base, spread) in spreads.items():
        noise = np.random.default_rng([zlib.crc32(name.encode()), seed]).standard_normal(out[name].shape)
        drawn = base * np.exp(spread * noise) if base else spread * noise
        out[name] = jnp.asarray(drawn.astype(out[name].dtype))
    for name, factor in factors.items():
        out[name] = (out[name] * factor).astype(out[name].dtype)
    return out
```

```python
from contextlib import ExitStack

import concourse.bass as bass
from concourse import mybir

ALU = mybir.AluOpType
ACT = mybir.ActivationFunctionType
AX = mybir.AxisListType
F32 = mybir.dt.float32
BF16 = mybir.dt.bfloat16
F16 = mybir.dt.float16
I32 = mybir.dt.int32
ds = bass.ds

P = 128
N = 1250
E = 20000
D = 768
R = 3
NT = (N + P - 1) // P
NP_ = NT * P
KT = D // P
LAST = N - (NT - 1) * P
EP, EC = 125, 160
assert EP * EC == E
PAIR = 2 * P
MAXPAIRS = (E + NT * (PAIR - 1)) // PAIR
PAIRS_STEP = 3
NPAIR = R * NT * PAIRS_STEP
assert NPAIR >= MAXPAIRS + 2
T = 2 * NPAIR
HALF = D // 2
RING = 3
ROW = D + 4
ROUND = 12582912.0
NEG = -1.5e38
EPS_LN = 1e-5
EPS_Z = 1e-16
SLOPE = 0.2


def gnn_kernel(nc, x, src, dst, edge_type, W0, b0, W1, q1, k1, b1, W2, q2, k2, b2, out, debug=None):
    HEADS = {1: 4, 2: 1}
    Wd = {1: W1, 2: W2}
    qd = {1: q1, 2: q2}
    kd = {1: k1, 2: k2}
    bd = {0: b0, 1: b1, 2: b2}

    WIDTH = {0: D + 1, 1: D + HEADS[1], 2: D + HEADS[2]}
    rows = {l: nc.dram_tensor(f"rows{l}", [NP_ if l == 0 else R * NP_, WIDTH[l]], F32).ap() for l in (0, 1, 2)}
    keys = {l: nc.dram_tensor(f"keys{l}", [R * NP_, HEADS[l]], F32).ap() for l in (1, 2)}

    with ExitStack() as ctx:
        def sb(name, shape, dt=F32):
            return ctx.enter_context(nc.sbuf_tensor(name, shape, dt))

        def sem(name):
            return ctx.enter_context(nc.semaphore(name))

        ps = ctx.enter_context(nc.psum_tensor("ps", [P, 8, 512], F32))
        psf = ps[:, :, :].rearrange("p b c -> p (b c)")

        xs = sb("xs", [P, NT, D])
        hT = sb("hT", [P, KT, NP_])
        wreg = sb("wreg", [P, 2, KT, D])
        hw0 = wreg[:, :, :, :].rearrange("p a k d -> p (a k d)")[:, 0:NT * D].rearrange("p (t d) -> p t d", t=NT)
        stT = sb("stT", [P, T * P], BF16)
        ring = sb("ring", [P, 2 * RING, ROW])
        ringf = ring[:, :, :].rearrange("p a d -> p (a d)")
        w0s = ringf[:, 0:KT * D].rearrange("p (k d) -> p k d", k=KT)
        hn = sb("hn", [P, 2, D])
        stage = sb("stage", [P, 2, ROW])
        zw = sb("zw", [P, 2, 2, 4, P])
        negm = hn[:, 0, 0:4 * P].rearrange("p (a b c) -> p a b c", a=2, b=2)
        s16 = sb("s16", [P, 2, P], BF16)
        bias = sb("bias", [P, D])
        etmp = sb("etmp", [P, D])
        mtm = etmp[:, 0:NPAIR * 4]
        qv = etmp[:, NPAIR * 4:NPAIR * 4 + NT * 2 * R * 4].rearrange("p (t q) -> p t q", t=NT)

        stf = stT[:, :].bitcast(F32)
        at = [0]

        def temp(words, dt=F32, parts=P):
            v = stf[0:parts, at[0]:at[0] + words]
            at[0] += words
            assert at[0] <= T * P // 2
            return v if dt == F32 else v.bitcast(dt)

        e_i = temp(3 * EC, I32, EP).rearrange("p (a c) -> p a c", a=3)
        e_f = temp(3 * EC, F32, EP).rearrange("p (a c) -> p a c", a=3)
        dtile = temp(EC, F32, EP)
        dloc = temp(EC, F32, EP)
        t_a = temp(EC, F32, EP)
        t_b = temp(EC, F32, EP)
        field1 = temp(EC, F32, EP)
        field2 = temp(EC, F32, EP)
        slot_hi = temp(EC, F32, EP)
        slot_lo = temp(EC, F32, EP)
        bucket = temp(NT * EC // 2, BF16, EP).rearrange("p (j c) -> p j c", j=NT)
        cumA = temp(NT * EC // 2, BF16, EP).rearrange("p (j c) -> p j c", j=NT)
        cumB = temp(NT * EC // 2, BF16, EP).rearrange("p (j c) -> p j c", j=NT)
        wpos = temp(NT * EC, F32, EP).rearrange("p (j c) -> p j c", j=NT)
        upper = temp(P, F32, EP)
        ones = temp(P, F32, EP)
        rowtot = temp(NT, F32, EP)
        PB = 4
        oh_lo = temp(PB * P // 2, F16, EP).rearrange("p (b c) -> p b c", b=PB)
        oh_tg = temp(PB * P // 2, F16, EP).rearrange("p (b c) -> p b c", b=PB)
        oh_hi = temp(PB * T, F16, EP).rearrange("p (b f c) -> p b f c", b=PB, f=2)
        wt = [temp(D) for _ in range(2)]

        iota_f = sb("iota_f", [P, T])
        iota_h = sb("iota_h", [P, T], F16)
        iota_p = sb("iota_p", [P, 1])
        ident = sb("ident", [P, P])
        ident16 = sb("ident16", [P, P], BF16)
        zero16 = sb("zero16", [P, HALF + 2], BF16)
        half = sb("half", [P, NT])
        wqk = {l: sb(f"wqk{l}", [P, KT, 2, R * HEADS[l]]) for l in (1, 2)}
        qk = {l: sb(f"qk{l}", [P, KT, 2, HEADS[l]]) for l in (1, 2)}
        al = sb("al", [P, T * 4])
        fields = al[:, 0:2 * T].rearrange("p (f c) -> p f c", f=2)
        t_r = al[:, 2 * T:3 * T]
        t_s = al[:, 3 * T:4 * T]
        tl = sb("tl", [P, T])
        idx0 = sb("idx0", [P, T], I32)
        idxr = sb("idxr", [P, T], I32)
        idxs = sb("idxs", [P, 2 * RING], I32)
        kidx = sb("kidx", [P, 2, 2 * PAIRS_STEP], I32)
        rmask = sb("rmask", [P, T, R])
        pj = sb("pj", [P, NT, NPAIR])
        tot = sb("tot", [P, NT])
        cnt = sb("cnt", [P, NT])
        pstart = sb("pstart", [P, 2, NT + 6])
        base = sb("base", [P, NT])
        bounds = sb("bounds", [P, NT + 1], I32)
        deg = sb("deg", [P, NT])
        dinv = sb("dinv", [P, NT])
        stats = sb("stats", [P, 2, 6])
        mv = sb("mv", [P, NT, 2])
        vare = sb("vare", [P, NT])
        rstd = sb("rstd", [P, NT])
        kst = sb("kst", [P, R, NT, 4])
        q16 = sb("q16", [P, NT, 3, R * 4], BF16)
        m16 = sb("m16", [P, NT, 3, 4], BF16)
        mx = sb("mx", [P, NT, 4])
        mxr = sb("mxr", [P, NT, 4])
        kb = sb("kb", [P, 2, 2 * PAIRS_STEP, 4])
        qs = sb("qs", [P, T * 4])
        me = qs
        atmp = sb("atmp", [P, 2 * PAIRS_STEP * 4])
        mt = sb("mt", [P, NPAIR * 4])
        z = sb("z", [P, 4])
        rz = sb("rz", [P, 4])
        qe = ringf[:, 0:T * R * 4]

        s_x = [sem(f"s_x{i}") for i in range(4)]
        s_edges = sem("s_edges")
        s_w0 = sem("s_w0")
        s_qk = sem("s_qk")
        s_bias = [sem(f"s_bias{i}") for i in range(3)]
        wprep_in = [sem("wprep_in0"), sem("wprep_in1")]
        consts = sem("consts")
        pool_c = sem("pool_c")
        xpad = sem("xpad")
        t_ready, t_free = sem("t_ready"), sem("t_free")
        wt_used = sem("wt_used")
        wq_copied = sem("wq_copied")
        ranks_in, ranks_out = sem("ranks_in"), sem("ranks_out")
        bounds_ready = sem("bounds_ready")
        perm_in, perm_free = sem("perm_in"), sem("perm_free")
        slots_ready = sem("slots_ready")
        var_ready, rstd_ready = sem("var_ready"), sem("rstd_ready")
        deg_ready, dinv_ready = sem("deg_ready"), sem("dinv_ready")
        hn_ready = sem("hn_ready")
        p_ready = sem("p_ready")
        hw_ready = sem("hw_ready")
        dve_c = sem("dve_c")
        s_rows0 = sem("s_rows0")
        g_sem = {l: [sem(f"g{l}_{i}") for i in range(2 * RING)] for l in (0, 1, 2)}
        g_in = {l: sem(f"g_in{l}") for l in (0, 1, 2)}
        w_in = {l: sem(f"w_in{l}") for l in (0, 1, 2)}
        w_used = {l: sem(f"w_used{l}") for l in (0, 1, 2)}
        ix = sem("ix")
        turn = sem("turn")
        o16_in = sem("o16_in")
        st_ready, st_copied = sem("st_ready"), sem("st_copied")
        acc_free = {l: sem(f"acc_free{l}") for l in (0, 1, 2)}
        x1_ready = sem("x1_ready")
        s_w = {l: sem(f"s_w{l}") for l in (1, 2)}
        s_wb = {l: [sem(f"s_wb{l}_{i}") for i in range(2)] for l in (1, 2)}
        stage_in = {l: sem(f"stage_in{l}") for l in (1, 2)}
        stage_out = {l: [sem(f"stage_out{l}_{i}") for i in range(2)] for l in (1, 2)}
        qv_done = sem("qv_done")
        kst_ready, s_keys = sem("kst_ready"), sem("s_keys")
        q16_ready = sem("q16_ready")
        qe_done = {l: sem(f"qe_done{l}") for l in (1, 2)}
        qe_read = {l: sem(f"qe_read{l}") for l in (1, 2)}
        qs_ready = sem("qs_ready")
        k_in = {l: [sem(f"k_in{l}_{i}") for i in range(2)] for l in (1, 2)}
        k_used = {l: sem(f"k_used{l}") for l in (1, 2)}
        k_ix = sem("k_ix")
        al_step = {l: sem(f"al_step{l}") for l in (1, 2)}
        nm_step = {l: sem(f"nm_step{l}") for l in (1, 2)}
        z_in = {l: sem(f"z_in{l}") for l in (1, 2)}
        z_done = {l: sem(f"z_done{l}") for l in (1, 2)}
        z_read = {l: sem(f"z_read{l}") for l in (1, 2)}
        m16_ready = sem("m16_ready")
        me_done = {l: sem(f"me_done{l}") for l in (1, 2)}
        me_read = {l: sem(f"me_read{l}") for l in (1, 2)}
        al_ready, e_ready = sem("al_ready"), sem("e_ready")
        elu_in, elu_exp = sem("elu_in"), sem("elu_exp")
        rows_go = {l: sem(f"rows_go{l}") for l in (1, 2)}
        o_ready = sem("o_ready")
        s_out = sem("s_out")
        s_dbg = sem("s_dbg")

        NW = 2 * R * KT
        tbank = [2 * (n % 2) for n in range(NW + NT)] + [4 + 2 * (n % 2) for n in range(2 * NT)]

        def tbuf(n):
            return psf[:, tbank[n] * 512:tbank[n] * 512 + D]

        def load_bounds(eng):
            eng.wait_ge(bounds_ready, 1)
            return [0] + [eng.value_load(bounds[0:1, j:j + 1], min_val=j, max_val=MAXPAIRS) for j in range(1, NT + 1)]

        locals_ = dict(locals())
        block = ctx.enter_context(nc.Block())

        @block.sync
        def _(sp):
            for a, v in enumerate((src, dst, edge_type)):
                sp.dma_start(e_i[:, a, :], v.rearrange("(p c) -> p c", p=EP)).then_inc(s_edges, 16)
            for n in range(3):
                sp.dma_start(xs[:, 3 * n:3 * n + 3, :],
                             x[3 * n * P:(3 * n + 3) * P, :].rearrange("(t p) d -> p t d", p=P)).then_inc(s_x[n], 16)
            sp.wait_ge(xpad, 1)
            sp.dma_start(xs[0:LAST, NT - 1, :], x[(NT - 1) * P:N, :]).then_inc(s_x[3], 16)
            for l in (1, 2):
                for a, v in enumerate((qd[l], kd[l])):
                    with nc.allow_non_contiguous_dma(reason="small vectors"):
                        sp.dma_start(qk[l][:, :, a, :], v.rearrange("(t p) h -> p t h", p=P)).then_inc(s_qk, 16)
            sp.dma_start(bias[:, :], bd[0].partition_broadcast(P)).then_inc(s_bias[0], 16)
            n = 0
            for l in (1, 2):
                for r in range(R):
                    if n >= 2:
                        sp.wait_ge(wt_used, (n - 1) * KT)
                    sp.dma_start(wreg[:, n % 2, :, :], Wd[l][r].rearrange("(k p) n -> p k n", p=P)).then_inc(wprep_in[n % 2], 16)
                    n += 1
                    if n == 2:
                        sp.dma_start(w0s, W0.rearrange("(k p) n -> p k n", p=P)).then_inc(s_w0, 16)
            for nt in range(NT):
                sp.wait_ge(hw_ready, 2 * nt + 2)
                sp.dma_start(rows[0][nt * P:(nt + 1) * P, 0:D], hw0[:, nt, :]).then_inc(s_rows0, 16)
            sp.wait_ge(dinv_ready, 1)
            with nc.allow_non_contiguous_dma(reason="one column"):
                sp.dma_start(rows[0].rearrange("(t p) d -> p t d", p=P)[:, :, D:D + 1], dinv[:, :].unsqueeze(2)).then_inc(s_rows0, 16)
            bnd = load_bounds(sp)
            groups = (bnd[NT] + (RING - 1)) // RING

            def relay(l):
                sp.sem_inc(g_in[l], 1)
                with sp.Fori(0, groups) as g:
                    for s in range(2 * RING):
                        sp.wait_ge(g_sem[l][s], 16 * (g + 1))
                        sp.sem_inc(g_in[l], 1)

            relay(0)

            def load_weights(l, r):
                sp.dma_start(wreg[:, r % 2, :, :], Wd[l][r].rearrange("(k p) n -> p k n", p=P)).then_inc(s_wb[l][r % 2], 16)

            sp.wait_ge(x1_ready, NT)
            sp.dma_start(bias[:, :], bd[1].partition_broadcast(P)).then_inc(s_bias[1], 16)
            for l in (1, 2):
                if l == 1:
                    load_weights(1, 0)
                    load_weights(1, 1)
                for r in range(2):
                    sp.wait_ge(s_wb[l][r], 16)
                    sp.sem_inc(s_w[l], 1)
                sp.wait_ge(kst_ready, l)
                for r in range(R):
                    with nc.allow_non_contiguous_dma(reason="rows of keys"):
                        sp.dma_start(keys[l][r * NP_:(r + 1) * NP_, :].rearrange("(t p) h -> p t h", p=P),
                                     kst[:, r, :, 0:HEADS[l]]).then_inc(s_keys, 16)
                for r in range(R):
                    for nt in range(NT):
                        n = r * NT + nt
                        if n == NT + 1:
                            sp.wait_ge(p_ready, 2 * NT * (1 + R * (l - 1) + 1))
                            load_weights(l, 2)
                        if n == 2 * NT - 2:
                            sp.wait_ge(s_wb[l][0], 32)
                            sp.sem_inc(s_w[l], 1)
                        sp.wait_ge(stage_in[l], 4 + 2 * n + 2)
                        sp.dma_start(rows[l][r * NP_ + nt * P:r * NP_ + (nt + 1) * P, :], stage[:, nt % 2, 0:WIDTH[l]]).then_inc(stage_out[l][nt % 2], 16)
                if l == 1:
                    load_weights(2, 0)
                    load_weights(2, 1)
                relay(l)
                if l == 1:
                    sp.wait_ge(hn_ready, 3 * NT)
                    sp.dma_start(bias[:, :], bd[2].partition_broadcast(P)).then_inc(s_bias[2], 16)
            for j in range(NT):
                n = P if j < NT - 1 else LAST
                sp.wait_ge(o_ready, j + 1)
                sp.dma_start(out[j * P:j * P + n, :], xs[0:n, j, :]).then_inc(s_out, 16)
            sp.wait_ge(s_out, 16 * NT)
            if debug:
                pairs = debug(nc, locals_)
                for o, v in pairs:
                    sp.dma_start(o, v).then_inc(s_dbg, 16)
                sp.wait_ge(s_dbg, 16 * len(pairs))

        @block.gpsimd
        def _(pool):
            nc.gpsimd.iota(iota_f[:, :], [[1, T]], base=0, channel_multiplier=0, allow_small_or_imprecise_dtypes=True).then_inc(pool_c, 1)
            nc.gpsimd.iota(iota_h[:, :], [[1, T]], base=0, channel_multiplier=0, allow_small_or_imprecise_dtypes=True).then_inc(pool_c, 1)
            nc.gpsimd.iota(iota_p[:, :], [[0, 1]], base=0, channel_multiplier=1, allow_small_or_imprecise_dtypes=True).then_inc(pool_c, 1)
            nc.gpsimd.memset(half[:, :], -0.5).then_inc(pool_c, 1)
            nc.gpsimd.memset(zero16[:, :], 0.0).then_inc(pool_c, 1)
            nc.gpsimd.memset(ones[:, :], 1.0).then_inc(pool_c, 1)
            pool.wait_ge(pool_c, 6)
            pool.wait_ge(var_ready, 1)
            nc.gpsimd.tensor_tensor(rstd[:, :], vare[:, :], half[:, :], ALU.pow).then_inc(rstd_ready, 1)
            pool.wait_ge(deg_ready, 1)
            nc.gpsimd.tensor_tensor(dinv[:, :], deg[:, :], half[:, :], ALU.pow).then_inc(dinv_ready, 1)
            bnd = load_bounds(pool)
            groups = (bnd[NT] + (RING - 1)) // RING

            def gather_rows(l, idx, ix0):
                with pool.Fori(0, groups) as g:
                    pool.wait_ge(g_in[l], 2 * RING * g + 1)
                    nc.gpsimd.tensor_copy(idxs[:, :], idx[:, ds(g * (2 * RING), 2 * RING)]).then_inc(ix, 1)
                    pool.wait_ge(ix, g + (ix0 + 1))
                    pool.sem_inc(turn, 1)
                    for s in range(2 * RING):
                        if s % 2 == 0:
                            pool.wait_ge(w_used[l], g * (2 * RING) + (s + 2))
                            pool.sem_inc(turn, 1)
                        nc.gpsimd.indirect_dma_start(ring[:, s, 0:WIDTH[l]], None, rows[l], bass.IndirectOffsetOnAxis(idxs[:, s:s + 1], 0)).then_inc(g_sem[l][s], 16)

            pool.wait_ge(slots_ready, 1)
            pool.wait_ge(s_rows0, 16 * (NT + 1))
            gather_rows(0, idx0, 0)
            pool.wait_ge(var_ready, 2)
            nc.gpsimd.tensor_tensor(rstd[:, :], vare[:, :], half[:, :], ALU.pow).then_inc(rstd_ready, 1)
            ix_count = groups
            for l in (1, 2):
                pool.wait_ge(s_keys, 16 * R * l)
                pool.sem_inc(k_used[l], 2)
                with pool.Fori(0, R * NT // 2) as g:
                    for hf in range(2):
                        pool.wait_ge(k_used[l], 2 * g + (hf + 1))
                        nc.gpsimd.tensor_copy(kidx[:, hf, :], idxr[:, ds((2 * g + hf) * (2 * PAIRS_STEP), 2 * PAIRS_STEP)]).then_inc(k_ix, 1)
                        pool.wait_ge(k_ix, 2 * g + (hf + 1 + (l - 1) * R * NT))
                        pool.sem_inc(turn, 1)
                        for s in range(2 * PAIRS_STEP):
                            nc.gpsimd.indirect_dma_start(kb[:, hf, s, 0:HEADS[l]], None, keys[l], bass.IndirectOffsetOnAxis(kidx[:, hf, s:s + 1], 0)).then_inc(k_in[l][hf], 16)
                for hf in range(2):
                    pool.wait_ge(stage_out[l][hf], 16 * R * NT // 2)
                pool.wait_ge(rows_go[l], 1)
                gather_rows(l, idxr, ix_count)
                ix_count = ix_count + groups

        @block.scalar
        def _(act):
            def copy_t(n, out_ap, func=ACT.Copy):
                act.wait_ge(t_ready, n + 1)
                return nc.scalar.activation(out_ap, tbuf(n), func)

            for n in range(NW):
                if n >= 2:
                    act.wait_ge(wt_used, n - 1)
                copy_t(n, wt[n % 2]).then_inc(t_free, 1)
            for l in (1, 2):
                act.wait_ge(wt_used, l * R * KT)
                nc.scalar.activation(wqk[l][:, :, :, :],
                                     ps[:, 3 + l, 0:KT * 2 * R * HEADS[l]].rearrange("p (k a q) -> p k a q", k=KT, a=2), ACT.Copy).then_inc(wq_copied, 1)
            for nt in range(NT):
                n = NW + nt
                copy_t(n, hT[:, :, nt * P:(nt + 1) * P], ACT.Relu).then_inc(t_free, 1)
                if nt >= 1:
                    for h in range(2):
                        act.wait_ge(p_ready, 2 * (nt - 1) + h + 1)
                        nc.scalar.activation(hw0[:, nt - 1, h * HALF:(h + 1) * HALF], ps[:, 4 + h, 0:HALF], ACT.Copy).then_inc(hw_ready, 1)
            for h in range(2):
                act.wait_ge(p_ready, 2 * (NT - 1) + h + 1)
                nc.scalar.activation(hw0[:, NT - 1, h * HALF:(h + 1) * HALF], ps[:, 4 + h, 0:HALF], ACT.Copy).then_inc(hw_ready, 1)
            bnd = load_bounds(act)
            with act.Fori(0, bnd[NT]) as i:
                act.wait_ge(st_ready, i + 2)
                nc.scalar.activation(stT[:, ds(i * PAIR, PAIR)], ps[:, ds(i % 2 + 6, 1), 0:P].bitcast(BF16), ACT.Copy).then_inc(st_copied, 1)
            for l in (1, 2):
                H = HEADS[l]
                if l == 1:
                    for nt in range(NT):
                        copy_t(NW + NT + nt, hT[:, :, nt * P:(nt + 1) * P], ACT.Relu).then_inc(t_free, 1)
                for r in range(R):
                    for nt in range(NT):
                        b = nt % 2
                        if r * NT + nt >= 2:
                            act.wait_ge(stage_out[l][b], r * (16 * NT // 2) + 16 * (nt // 2))
                        for h in range(2):
                            act.wait_ge(p_ready, r * (2 * NT) + (2 * NT * (1 + R * (l - 1)) + 2 * nt + h + 1))
                            if H == 4:
                                o = stage[:, b, h * 2 * (HALF // 2 + 1):(h + 1) * 2 * (HALF // 2 + 1)].rearrange("p (a c) -> p a c", a=2)[:, :, 0:HALF // 2]
                                i_ = ps[:, 2 * b + h, 0:HALF].rearrange("p (a c) -> p a c", a=2)
                            else:
                                o = stage[:, b, h * HALF:(h + 1) * HALF]
                                i_ = ps[:, 2 * b + h, 0:HALF]
                            nc.scalar.activation(o, i_, ACT.Copy).then_inc(stage_in[l], 1)
                act.wait_ge(al_ready, l)
                nc.scalar.activation(al[:, 0:T * H], me[:, 0:T * H], ACT.Exp).then_inc(e_ready, 1)
                if l == 1:
                    for j in range(NT):
                        act.wait_ge(elu_in, j + 1)
                        nc.scalar.activation(etmp[:, :], etmp[:, :], ACT.Exp).then_inc(elu_exp, 1)
                        if j >= 1:
                            copy_t(NW + 2 * NT + j - 1, hT[:, :, (j - 1) * P:j * P]).then_inc(t_free, 1)
                    copy_t(NW + 3 * NT - 1, hT[:, :, (NT - 1) * P:NT * P]).then_inc(t_free, 1)

        @block.vector
        def _(dve):
            chain = [0]

            def link(ins):
                chain[0] += 1
                ins.then_inc(dve_c, 1)
                dve.wait_ge(dve_c, chain[0])

            V = nc.vector
            V.memset(xs[96:P, NT - 1, :], 0.0).then_inc(xpad, 1)
            dve.wait_ge(pool_c, 6)
            V.tensor_scalar(ident[:, :], iota_f[:, 0:P], iota_p[:, 0:1], None, ALU.is_equal).then_inc(consts, 1)
            V.tensor_scalar(ident16[:, :], iota_f[:, 0:P], iota_p[:, 0:1], None, ALU.is_equal).then_inc(consts, 1)
            V.tensor_scalar(upper[:, :], iota_f[0:EP, 0:P], iota_p[0:EP, 0:1], None, ALU.is_gt).then_inc(consts, 1)
            V.memset(stage[:, :, :], 1.0).then_inc(consts, 1)

            dve.wait_ge(s_edges, 48)
            link(V.tensor_copy(e_f, e_i))
            link(V.tensor_scalar(t_a, e_f[:, 1, :], 1.0 / P, -(P / 2 - 0.5) / P, ALU.mult, ALU.add))
            link(V.tensor_scalar(t_b, t_a, ROUND, None, ALU.add))
            link(V.tensor_scalar(dtile, t_b, -ROUND, None, ALU.add))
            link(V.scalar_tensor_tensor(dloc, dtile, -float(P), e_f[:, 1, :], ALU.mult, ALU.add))
            V.tensor_scalar(field1, e_f[:, 0, :], 1.0, None, ALU.add)
            link(V.tensor_scalar(t_a, dloc, 1.0, None, ALU.add))
            V.scalar_tensor_tensor(field2, e_f[:, 2, :], float(P), t_a, ALU.mult, ALU.add)
            for j in range(NT):
                last = V.tensor_scalar(bucket[:, j, :], dtile, float(j), None, ALU.is_equal)
            link(last)
            a, b, s = bucket, cumA, 1
            while s < EC:
                V.tensor_copy(b[:, :, 0:s], a[:, :, 0:s])
                link(V.tensor_tensor(b[:, :, s:EC], a[:, :, s:EC], a[:, :, 0:EC - s], ALU.add))
                a, b, s = b, (cumB if b is cumA else cumA), 2 * s
            cum = a
            V.tensor_copy(rowtot, cum[:, :, EC - 1]).then_inc(ranks_in, 1)
            dve.wait_ge(ranks_out, 1)
            link(V.tensor_scalar(cnt[:, :], ps[:, 7, NT:2 * NT], 1.0 / PAIR, (PAIR / 2 - 0.5) / PAIR, ALU.mult, ALU.add))
            link(V.tensor_scalar(tot[:, :], cnt[:, :], ROUND, None, ALU.add))
            V.memset(pstart[:, :, :], 0.0)
            link(V.tensor_scalar(cnt[:, :], tot[:, :], -ROUND, None, ALU.add))
            link(V.tensor_scalar(pstart[:, 0, 1:NT + 1], cnt[:, :], 1.0, None, ALU.max))
            u, s = 0, 1
            while s < NT:
                V.tensor_copy(pstart[:, 1 - u, 1:s + 1], pstart[:, u, 1:s + 1])
                link(V.tensor_tensor(pstart[:, 1 - u, s + 1:NT + 1], pstart[:, u, s + 1:NT + 1], pstart[:, u, 1:NT + 1 - s], ALU.add))
                u, s = 1 - u, 2 * s
            V.tensor_copy(bounds[:, :], pstart[:, u, 0:NT + 1]).then_inc(bounds_ready, 1)
            link(V.scalar_tensor_tensor(base[:, :], pstart[:, u, 0:NT], float(PAIR), ps[:, 7, 0:NT], ALU.mult, ALU.add))
            link(V.tensor_scalar(base[:, :], base[:, :], -1.0, None, ALU.add))
            link(V.tensor_tensor(wpos, cum, base[0:EP, :].unsqueeze(2).to_broadcast([EP, NT, EC]), ALU.add))
            link(V.tensor_tensor(wpos, wpos, bucket, ALU.mult))
            link(V.tensor_reduce(t_a, wpos.rearrange("p j c -> p c j"), AX.X, ALU.add))
            link(V.tensor_scalar(t_b, t_a, 1.0 / P, -(P / 2 - 0.5) / P, ALU.mult, ALU.add))
            link(V.tensor_scalar(t_b, t_b, ROUND, None, ALU.add))
            link(V.tensor_scalar(slot_hi, t_b, -ROUND, None, ALU.add))
            link(V.scalar_tensor_tensor(slot_lo, slot_hi, -float(P), t_a, ALU.mult, ALU.add))
            dve.wait_ge(ranks_out, 1)
            for j in range(NT):
                link(V.tensor_scalar(pj[:, j, :], iota_f[:, 0:NPAIR], pstart[:, u, j:j + 1], NEG, ALU.is_lt, ALU.mult))
                link(V.tensor_scalar(mtm[:, 0:NPAIR], iota_f[:, 0:NPAIR], pstart[:, u, j + 1:j + 2], NEG, ALU.is_ge, ALU.mult))
                link(V.tensor_tensor(pj[:, j, :], pj[:, j, :], mtm[:, 0:NPAIR], ALU.add))

            def moments(j):
                V.bn_stats(stats[:, 0, :], xs[:, j, 0:HALF])
                link(V.bn_stats(stats[:, 1, :], xs[:, j, HALF:D]))
                link(V.bn_aggr(mv[:, j, :], stats[:, :, :].rearrange("p a c -> p (a c)")))

            for j in range(NT):
                if j % 3 == 0:
                    dve.wait_ge(s_x[j // 3], 16)
                if j == NT - 1:
                    dve.wait_ge(xpad, 1)
                moments(j)
            V.tensor_scalar(vare[:, :], mv[:, :, 1], EPS_LN, None, ALU.add).then_inc(var_ready, 1)
            dve.wait_ge(rstd_ready, 1)

            def edge_columns(c0):
                for b in range(PB):
                    dve.wait_ge(perm_free, c0 + (b + 1))
                    V.tensor_scalar(oh_lo[:, b, :], iota_h[0:EP, 0:P], slot_lo[:, ds(c0 + b, 1)], None, ALU.is_equal)
                    V.tensor_scalar(oh_tg[:, b, :], iota_h[0:EP, 0:P], dloc[:, ds(c0 + b, 1)], None, ALU.is_equal)
                    V.tensor_scalar(oh_hi[:, b, 0, :], iota_h[0:EP, :], slot_hi[:, ds(c0 + b, 1)], field1[:, ds(c0 + b, 1)], ALU.is_equal, ALU.mult)
                    V.tensor_scalar(oh_hi[:, b, 1, :], iota_h[0:EP, :], slot_hi[:, ds(c0 + b, 1)], field2[:, ds(c0 + b, 1)], ALU.is_equal, ALU.mult).then_inc(perm_in, 1)

            for j in range(NT):
                if j >= 2:
                    dve.wait_ge(t_ready, NW + j - 1)
                V.tensor_scalar(hn[:, j % 2, :], xs[:, j, :], mv[:, j, 0:1], rstd[:, j:j + 1], ALU.subtract, ALU.mult).then_inc(hn_ready, 1)
                with dve.Fori(j * (EC // NT // PB), (j + 1) * (EC // NT // PB)) as c:
                    edge_columns(PB * c)
            dve.wait_ge(perm_free, EC + PB)
            V.tensor_scalar(deg[:, :], ps[:, 7, 0:NT], 1.0, None, ALU.add).then_inc(deg_ready, 1)
            link(V.tensor_copy(fields[:, :, :], ps[:, 6, 0:2 * T].rearrange("p (f c) -> p f c", f=2)))
            link(V.tensor_scalar(t_s[:, :], fields[:, 0, :], -1.0, 0.0, ALU.add, ALU.max))
            V.tensor_copy(idx0[:, :], t_s[:, :])
            link(V.tensor_scalar(t_r[:, :], fields[:, 1, :], 1.0 / P, -(P / 2 + 0.5) / P, ALU.mult, ALU.add))
            link(V.tensor_scalar(t_r[:, :], t_r[:, :], ROUND, None, ALU.add))
            link(V.tensor_scalar(t_r[:, :], t_r[:, :], -ROUND, 0.0, ALU.add, ALU.max))
            link(V.scalar_tensor_tensor(tl[:, :], t_r[:, :], -float(P), fields[:, 1, :], ALU.mult, ALU.add))
            link(V.tensor_scalar(tl[:, :], tl[:, :], -1.0, None, ALU.add))
            for r in range(R):
                V.tensor_scalar(rmask[:, :, r], t_r[:, :], float(r), None, ALU.is_equal)
            link(V.scalar_tensor_tensor(t_s[:, :], t_r[:, :], float(NP_), t_s[:, :], ALU.mult, ALU.add))
            V.tensor_copy(idxr[:, :], t_s[:, :]).then_inc(slots_ready, 1)
            dve.wait_ge(slots_ready, 1)
            bnd = load_bounds(dve)
            groups = (bnd[NT] + (RING - 1)) // RING

            def finish0(j):
                dve.wait_ge(w_used[0], 2 * bnd[j + 1] + 2 * RING)
                if j == 0:
                    dve.wait_ge(dinv_ready, 1)
                    dve.wait_ge(s_bias[0], 16)
                bk = 2 * (j % 2)
                link(V.scalar_tensor_tensor(etmp[:, :].rearrange("p (a c) -> p a c", a=2), hw0[:, j, :].rearrange("p (a c) -> p a c", a=2), dinv[:, j:j + 1], ps[:, bk:bk + 2, 0:HALF], ALU.mult, ALU.add))
                dve.sem_inc(acc_free[0], 1)
                link(V.scalar_tensor_tensor(xs[:, j, :], etmp[:, :], dinv[:, j:j + 1], xs[:, j, :], ALU.mult, ALU.add))
                V.tensor_tensor(xs[:, j, :], xs[:, j, :], bias[:, :], ALU.add).then_inc(x1_ready, 1)
                dve.wait_ge(x1_ready, j + 1)
                moments(j)

            for j in range(NT):
                with dve.Fori(bnd[j], bnd[j + 1]) as i:
                    for b in range(2):
                        t = 2 * i + b
                        if b == 0:
                            dve.wait_ge(st_ready, i + 1)
                        V.tensor_scalar(s16[:, b, :], iota_h[:, 0:P], tl[:, ds(t, 1)], None, ALU.is_equal).then_inc(o16_in, 1)
                        dve.wait_ge(g_in[0], t + 2)
                        dve.wait_ge(w_used[0], t + (2 * RING - 1))
                        V.tensor_scalar(zw[:, 0, b, 0, :], iota_f[:, 0:P], tl[:, ds(t, 1)], ring[:, ds((i % RING) * 2 + b, 1), D:D + 1].rearrange("p a c -> p (a c)"), ALU.is_equal, ALU.mult).then_inc(w_in[0], 1)
                if j >= 1:
                    finish0(j - 1)
            finish0(NT - 1)
            V.tensor_scalar(vare[:, :], mv[:, :, 1], EPS_LN, None, ALU.add).then_inc(var_ready, 1)

            for l in (1, 2):
                H = HEADS[l]
                if l == 1:
                    dve.wait_ge(rstd_ready, 2)
                    for j in range(NT):
                        dve.wait_ge(t_ready, NW + NT + j - 1)
                        V.tensor_scalar(hn[:, j % 2, :], xs[:, j, :], mv[:, j, 0:1], rstd[:, j:j + 1], ALU.subtract, ALU.mult).then_inc(hn_ready, 1)
                if l == 2:
                    dve.wait_ge(s_keys, 16 * R)
                    for b in range(2):
                        dve.wait_ge(stage_out[1][b], 16 * R * NT // 2)
                    V.memset(stage[:, :, D:D + 1], 1.0)
                dve.wait_ge(qv_done, l)
                V.tensor_copy(kst[:, :, :, 0:H], ps[:, 0, 0:NT * 2 * R * H].rearrange("p (t a r h) -> p a r t h", t=NT, a=2, r=R)[:, 1]).then_inc(kst_ready, 1)
                link(V.tensor_copy(qv[:, :, 0:R * H], ps[:, 0, 0:NT * 2 * R * H].rearrange("p (t a q) -> p a t q", t=NT, a=2)[:, 0]))
                for part in range(3):
                    link(V.tensor_copy(q16[:, :, part, 0:R * H], qv[:, :, 0:R * H]))
                    if part < 2:
                        link(V.tensor_tensor(qv[:, :, 0:R * H], qv[:, :, 0:R * H], q16[:, :, part, 0:R * H], ALU.subtract))
                dve.sem_inc(q16_ready, 1)
                dve.wait_ge(g_in[l - 1], 2 * RING * groups + 1)
                link(V.memset(qe[:, 0:T * R * H], 0.0))
                with dve.Fori(0, bnd[NT]) as i:
                    dve.wait_ge(qe_done[l], i + 1)
                    V.tensor_reduce(qe[:, ds(i * (2 * R * H), 2 * R * H)].rearrange("p (b q) -> p b q", b=2),
                                    ps[:, ds(i % 2 + 2, 1), 0:2 * 3 * R * H].rearrange("p o (b c q) -> p (o b) q c", b=2, c=3), AX.X, ALU.add).then_inc(qe_read[l], 1)
                dve.wait_ge(qe_read[l], bnd[NT] + 2)
                qe3 = qe[:, 0:T * R * H].rearrange("p (t h) -> p t h", h=H)
                link(V.tensor_tensor(qe3, qe3, rmask[:, :, :].rearrange("p t r -> p (t r)").unsqueeze(2).to_broadcast([P, T * R, H]), ALU.mult))
                V.tensor_reduce(qs[:, 0:T * H].rearrange("p (t h) -> p t h", h=H), qe[:, 0:T * R * H].rearrange("p (t r h) -> p t h r", r=R, h=H), AX.X, ALU.add).then_inc(rows_go[l], 1)
                dve.wait_ge(rows_go[l], 1)

                dve.sem_inc(z_in[l], 1)
                def maxima(r, n):
                    bk = 4 + 2 * (n % 2)
                    dve.wait_ge(z_done[l], r * (NT * PAIRS_STEP) + (n + 1))
                    V.tensor_reduce(mt[:, ds(r * (NT * PAIRS_STEP * H) + n * H, H)],
                                    psf[:, bk * 512:bk * 512 + 2 * H * P].rearrange("p (b h e) -> p h b e", b=2, h=H), AX.XY, ALU.max).then_inc(z_read[l], 1)

                with dve.Fori(0, R) as r:
                    for nt in range(NT):
                        hf = nt % 2
                        C = 2 * PAIRS_STEP
                        at_ = r * (NT * C * H) + nt * C * H
                        dve.wait_ge(k_in[l][hf], r * (16 * C * NT // 2) + 16 * C * (nt // 2 + 1))
                        V.tensor_tensor(atmp[:, 0:C * H].rearrange("p (c h) -> p c h", h=H), qs[:, ds(at_, C * H)].rearrange("p (c h) -> p c h", h=H), kb[:, hf, :, 0:H], ALU.add).then_inc(k_used[l], 1)
                        dve.wait_ge(k_used[l], r * NT + (nt + 3))
                        V.scalar_tensor_tensor(al[:, ds(at_, C * H)], atmp[:, 0:C * H], SLOPE, atmp[:, 0:C * H], ALU.mult, ALU.max).then_inc(al_step[l], 1)
                        dve.wait_ge(al_step[l], r * NT + (nt + 1))
                        for k in range(PAIRS_STEP):
                            n = nt * PAIRS_STEP + k
                            dve.wait_ge(z_in[l], r * (NT * PAIRS_STEP) + max(n, 1))
                            for b in range(2):
                                tt = r * (NT * C) + (nt * C + 2 * k + b)
                                V.tensor_scalar(negm[:, n % 2, b, :], iota_f[:, 0:P], tl[:, ds(tt, 1)], NEG, ALU.not_equal, ALU.mult).then_inc(nm_step[l], 1)
                            for b in range(2):
                                tt = r * (NT * C) + (nt * C + 2 * k + b)
                                dve.wait_ge(nm_step[l], r * (2 * NT * PAIRS_STEP) + (2 * n + b + 1))
                                for h in range(H):
                                    last = V.tensor_scalar(zw[:, n % 2, b, h, :], negm[:, n % 2, b, :], al[:, ds(tt * H + h, 1)], None, ALU.add)
                            last.then_inc(z_in[l], 1)
                            if n >= 1:
                                maxima(r, n - 1)
                    maxima(r, NT * PAIRS_STEP - 1)
                dve.wait_ge(z_read[l], NPAIR + 2)
                for j in range(NT):
                    m3 = mtm[:, 0:NPAIR * H].rearrange("p (h i) -> p h i", h=H)
                    link(V.tensor_tensor(m3, mt[:, 0:NPAIR * H].rearrange("p (i h) -> p h i", h=H), pj[:, j, :].unsqueeze(1).to_broadcast([P, H, NPAIR]), ALU.add))
                    link(V.tensor_reduce(mx[:, j, 0:H], m3, AX.X, ALU.max))
                link(V.tensor_copy(mxr[:, :, 0:H], mx[:, :, 0:H]))
                for part in range(3):
                    link(V.tensor_copy(m16[:, :, part, 0:H], mxr[:, :, 0:H]))
                    if part < 2:
                        link(V.tensor_tensor(mxr[:, :, 0:H], mxr[:, :, 0:H], m16[:, :, part, 0:H], ALU.subtract))
                link(V.memset(me[:, 0:T * H], 0.0))
                dve.sem_inc(m16_ready, 1)
                with dve.Fori(0, bnd[NT]) as i:
                    dve.wait_ge(me_done[l], i + 1)
                    V.tensor_reduce(me[:, ds(i * (2 * H), 2 * H)].rearrange("p (b q) -> p b q", b=2),
                                    ps[:, ds(i % 2, 1), 0:2 * 3 * H].rearrange("p o (b c q) -> p (o b) q c", b=2, c=3), AX.X, ALU.add).then_inc(me_read[l], 1)
                dve.wait_ge(me_read[l], bnd[NT] + 2)
                link(V.tensor_tensor(me[:, 0:T * H], al[:, 0:T * H], me[:, 0:T * H], ALU.subtract))
                V.tensor_scalar(me[:, 0:T * H], me[:, 0:T * H], 0.0, None, ALU.min).then_inc(al_ready, 1)
                dve.wait_ge(e_ready, l)

                def finish(j):
                    dve.wait_ge(w_used[l], 2 * bnd[j + 1] + 2 * RING)
                    if j == 0:
                        dve.wait_ge(s_bias[l], 16)
                    bk = 2 * (j % 2)
                    W = HALF // 2 + 1
                    if l == 1:
                        zs = ps[:, bk:bk + 2, 0:2 * W].rearrange("p a (b c) -> p a b c", b=2)[:, :, :, W - 1]
                        link(V.tensor_scalar(z[:, 0:4].rearrange("p (a b) -> p a b", a=2), zs, EPS_Z, None, ALU.add))
                        link(V.reciprocal(rz[:, :], z[:, :]))
                        dve.wait_ge(t_ready, NW + 2 * NT + j - 1)
                        for h in range(4):
                            o = slice(h * (D // 4), (h + 1) * (D // 4))
                            last = V.scalar_tensor_tensor(hn[:, j % 2, o], ps[:, bk + h // 2, (h % 2) * W:(h % 2) * W + D // 4], rz[:, h:h + 1], bias[:, o], ALU.mult, ALU.add)
                        link(last)
                        if j >= 1:
                            dve.wait_ge(elu_exp, j)
                        dve.sem_inc(acc_free[l], 1)
                        V.tensor_scalar(etmp[:, :], hn[:, j % 2, :], 0.0, None, ALU.min).then_inc(elu_in, 1)
                        dve.wait_ge(elu_exp, j + 1)
                        V.scalar_tensor_tensor(hn[:, j % 2, :], etmp[:, :], -1.0, hn[:, j % 2, :], ALU.add, ALU.max).then_inc(hn_ready, 1)
                    else:
                        link(V.tensor_scalar(z[:, 0:1], ps[:, bk + 1, HALF:HALF + 1], EPS_Z, None, ALU.add))
                        link(V.reciprocal(rz[:, 0:1], z[:, 0:1]))
                        link(V.scalar_tensor_tensor(xs[:, j, :].rearrange("p (a c) -> p a c", a=2), ps[:, bk:bk + 2, 0:HALF], rz[:, 0:1], xs[:, j, :].rearrange("p (a c) -> p a c", a=2), ALU.mult, ALU.add))
                        dve.sem_inc(acc_free[l], 1)
                        V.tensor_tensor(xs[:, j, :], xs[:, j, :], bias[:, :], ALU.add).then_inc(o_ready, 1)

                for j in range(NT):
                    with dve.Fori(bnd[j], bnd[j + 1]) as i:
                        for b in range(2):
                            t = 2 * i + b
                            dve.wait_ge(w_used[l], t + (2 * RING - 1))
                            for h in range(H):
                                last = V.tensor_scalar(zw[:, 0, b, h, :], iota_f[:, 0:P], tl[:, ds(t, 1)], al[:, ds(t * H + h, 1)], ALU.is_equal, ALU.mult)
                            last.then_inc(w_in[l], 1)
                    if j >= 1:
                        finish(j - 1)
                finish(NT - 1)

        @block.tensor
        def _(pe):
            mm = nc.tensor.matmul

            def transposes(n, tile):
                for k in range(KT):
                    last = nc.tensor.transpose(tbuf(n)[:, k * P:(k + 1) * P], tile(k), ident[:, :])
                last.then_inc(t_ready, 1)

            pe.wait_ge(consts, 4)
            pe.wait_ge(s_qk, 64)
            tiles = [(l, r, k) for l in (1, 2) for r in range(R) for k in range(KT)]

            def wq_tile(n):
                l, r, k = tiles[n]
                H = HEADS[l]
                pe.wait_ge(t_free, n + 1)
                o = ps[:, 3 + l, 0:KT * 2 * R * H].rearrange("p (k a r h) -> p k a r h", k=KT, a=2, r=R)[:, k, :, r, :]
                for f in range(KT):
                    last = mm(o, wt[n % 2][:, f * P:(f + 1) * P], qk[l][:, f, :, :], start=(f == 0), stop=(f == KT - 1))
                last.then_inc(wt_used, 1)

            for n, (l, r, k) in enumerate(tiles):
                if n >= 2:
                    pe.wait_ge(t_free, n - 1)
                if k == 0:
                    pe.wait_ge(wprep_in[(n // KT) % 2], 16 * (n // KT // 2 + 1))
                transposes(n, lambda f: wreg[:, (n // KT) % 2, k, f * P:(f + 1) * P])
                if n >= 1:
                    wq_tile(n - 1)
            wq_tile(NW - 1)

            pe.wait_ge(ranks_in, 1)
            mm(ps[:, 7, 0:NT], upper[:, :], rowtot, start=True, stop=True)
            mm(ps[:, 7, NT:2 * NT], ones[:, :], rowtot, start=True, stop=True).then_inc(ranks_out, 1)

            pe.wait_ge(s_w0, 16)
            pe.wait_ge(wq_copied, 2)
            pe.sem_inc(perm_free, PB)
            for nt in range(NT):
                n = NW + nt
                pe.wait_ge(hn_ready, nt + 1)
                pe.wait_ge(t_free, n - 1)
                for k in range(KT):
                    last = nc.tensor.transpose(tbuf(n)[:, k * P:(k + 1) * P], hn[:, nt % 2, k * P:(k + 1) * P], ident[:, :])
                last.then_inc(t_ready, 1)
                if nt == 0:
                    pe.wait_ge(perm_in, 1)
                    mm(ps[:, 6, 0:2 * T], zero16[0:EP, 0:P], zero16[0:EP, 0:2 * T], start=True, stop=False, skip_group_check=True)
                    mm(ps[:, 7, 0:NT], zero16[0:EP, 0:P], zero16[0:EP, 0:NT], start=True, stop=False, skip_group_check=True)
                with pe.Fori(nt * (EC // NT // PB), (nt + 1) * (EC // NT // PB)) as g:
                    c = PB * g
                    for b in range(PB):
                        pe.wait_ge(perm_in, c + (b + 1))
                        mm(ps[:, 6, 0:2 * T], oh_lo[:, b, :], oh_hi[:, b, :, :].rearrange("p f c -> p (f c)"), start=False, stop=False, skip_group_check=True)
                        mm(ps[:, 7, 0:NT], oh_tg[:, b, :], bucket[:, :, ds(c + b, 1)].rearrange("p j c -> p (j c)"), start=False, stop=False, skip_group_check=True).then_inc(perm_free, 1)
                pe.wait_ge(t_free, n + 1)
                for h in range(2):
                    if nt >= 1:
                        pe.wait_ge(hw_ready, 2 * (nt - 1) + h + 1)
                    for k in range(KT):
                        last = mm(ps[:, 4 + h, 0:HALF], hT[:, k, nt * P:(nt + 1) * P], w0s[:, k, h * HALF:(h + 1) * HALF], start=(k == 0), stop=(k == KT - 1))
                    last.then_inc(p_ready, 1)

            bnd = load_bounds(pe)

            def open_acc(l, j):
                if j >= 2:
                    pe.wait_ge(acc_free[l], j - 1)
                for a in range(2):
                    mm(ps[:, 2 * (j % 2) + a, 0:HALF + 2], zero16[:, 0:P], zero16[:, :], start=True, stop=False, skip_group_check=True)

            pe.sem_inc(w_used[0], 2 * RING)
            pe.sem_inc(st_copied, 2)
            pe.sem_inc(st_ready, 1)
            for j in range(NT):
                open_acc(0, j)
                with pe.Fori(bnd[j], bnd[j + 1]) as i:
                    pe.wait_ge(o16_in, 2 * i + 2)
                    pe.wait_ge(st_copied, i + 1)
                    for b in range(2):
                        last = nc.tensor.transpose(ps[:, ds(i % 2 + 6, 1), 0:P].bitcast(BF16).rearrange("p o c -> p (o c)")[:, b * P:(b + 1) * P], s16[:, b, :], ident16[:, :])
                    last.then_inc(st_ready, 1)
                    for b in range(2):
                        pe.wait_ge(w_in[0], 2 * i + (b + 1))
                        for a in range(2):
                            last = mm(ps[:, 2 * (j % 2) + a, 0:HALF], zw[:, 0, b, 0, :], ring[:, ds((i % RING) * 2 + b, 1), a * HALF:(a + 1) * HALF].rearrange("p o c -> p (o c)"), start=False, stop=False, skip_group_check=True)
                        last.then_inc(w_used[0], 1)

            for l in (1, 2):
                H = HEADS[l]
                if l == 1:
                    pe.wait_ge(st_copied, bnd[NT] + 2)
                    for nt in range(NT):
                        n = NW + NT + nt
                        pe.wait_ge(hn_ready, NT + nt + 1)
                        pe.wait_ge(t_free, n - 1)
                        for k in range(KT):
                            last = nc.tensor.transpose(tbuf(n)[:, k * P:(k + 1) * P], hn[:, nt % 2, k * P:(k + 1) * P], ident[:, :])
                        last.then_inc(t_ready, 1)
                pe.wait_ge(t_free, NW + (l + 1) * NT)
                pe.wait_ge(acc_free[l - 1], NT)
                for nt in range(NT):
                    for k in range(KT):
                        last = mm(ps[:, 0, nt * 2 * R * H:(nt + 1) * 2 * R * H], hT[:, k, nt * P:(nt + 1) * P], wqk[l][:, k, :, :].rearrange("p a q -> p (a q)"), start=(k == 0), stop=(k == KT - 1))
                last.then_inc(qv_done, 1)
                pe.wait_ge(q16_ready, l)
                pe.sem_inc(qe_read[l], 2)
                for j in range(NT):
                    with pe.Fori(bnd[j], bnd[j + 1]) as i:
                        pe.wait_ge(qe_read[l], i + 1)
                        for b in range(2):
                            last = mm(ps[:, ds(i % 2 + 2, 1), b * 3 * R * H:(b + 1) * 3 * R * H].rearrange("p o (c q) -> p (o c) q", c=3), stT[:, ds((2 * i + b) * P, P)], q16[:, j, :, 0:R * H], start=True, stop=True)
                        last.then_inc(qe_done[l], 1)
                pe.wait_ge(qe_read[l], bnd[NT] + 2)
                pe.sem_inc(z_read[l], 2)
                pe.sem_inc(stage_in[l], 4)
                with pe.Fori(0, R) as r:
                    for nt in range(NT):
                        if nt == 0:
                            pe.wait_ge(s_w[l], r + 1)
                        for h in range(2):
                            pe.wait_ge(stage_in[l], r * (2 * NT) + (2 * nt + h + 1))
                            for k in range(KT):
                                last = mm(ps[:, 2 * (nt % 2) + h, 0:HALF], hT[:, k, nt * P:(nt + 1) * P], wreg[:, ds(r % 2, 1), k, h * HALF:(h + 1) * HALF].rearrange("p o c -> p (o c)"), start=(k == 0), stop=(k == KT - 1))
                            last.then_inc(p_ready, 1)
                        for k in range(PAIRS_STEP):
                            n = nt * PAIRS_STEP + k
                            pe.wait_ge(z_in[l], r * (NT * PAIRS_STEP) + (n + 2))
                            pe.wait_ge(z_read[l], r * (NT * PAIRS_STEP) + (n + 1))
                            bk = 4 + 2 * (n % 2)
                            for b in range(2):
                                for h in range(H):
                                    c = bk * 512 + (b * H + h) * P
                                    last = nc.tensor.transpose(psf[:, c:c + P], zw[:, n % 2, b, h, :], ident[:, :])
                            last.then_inc(z_done[l], 1)
                pe.wait_ge(m16_ready, l)
                pe.wait_ge(stage_in[l], 4 + 2 * R * NT)
                pe.sem_inc(me_read[l], 2)
                for j in range(NT):
                    with pe.Fori(bnd[j], bnd[j + 1]) as i:
                        pe.wait_ge(me_read[l], i + 1)
                        for b in range(2):
                            last = mm(ps[:, ds(i % 2, 1), b * 3 * H:(b + 1) * 3 * H].rearrange("p o (c q) -> p (o c) q", c=3), stT[:, ds((2 * i + b) * P, P)], m16[:, j, :, 0:H], start=True, stop=True)
                        last.then_inc(me_done[l], 1)
                pe.wait_ge(me_read[l], bnd[NT] + 2)
                pe.sem_inc(w_used[l], 2 * RING)
                for j in range(NT + 1):
                    if j < NT:
                        open_acc(l, j)
                        with pe.Fori(bnd[j], bnd[j + 1]) as i:
                            for b in range(2):
                                pe.wait_ge(w_in[l], 2 * i + (b + 1))
                                pe.wait_ge(g_in[l], 2 * i + (b + 2))
                                row = ring[:, ds((i % RING) * 2 + b, 1), :].rearrange("p o c -> p (o c)")
                                W = HALF // 2 + 1
                                if H == 4:
                                    for h in range(H):
                                        last = mm(ps[:, 2 * (j % 2) + h // 2, (h % 2) * W:(h % 2 + 1) * W], zw[:, 0, b, h, :], row[:, h * W:(h + 1) * W], start=False, stop=False, skip_group_check=True)
                                else:
                                    mm(ps[:, 2 * (j % 2), 0:HALF], zw[:, 0, b, 0, :], row[:, 0:HALF], start=False, stop=False, skip_group_check=True)
                                    last = mm(ps[:, 2 * (j % 2) + 1, 0:HALF + 1], zw[:, 0, b, 0, :], row[:, HALF:D + 1], start=False, stop=False, skip_group_check=True)
                                last.then_inc(w_used[l], 1)
                    if l == 1 and j >= 2:
                        for nt in ([j - 2] if j < NT else [j - 2, j - 1]):
                            n = NW + 2 * NT + nt
                            pe.wait_ge(hn_ready, 2 * NT + nt + 1)
                            pe.wait_ge(t_free, n - 1)
                            for k in range(KT):
                                last = nc.tensor.transpose(tbuf(n)[:, k * P:(k + 1) * P], hn[:, nt % 2, k * P:(k + 1) * P], ident[:, :])
                            last.then_inc(t_ready, 1)


_INS = ['x', 'src', 'dst', 'edge_type_3', 'L0_gnn_W', 'L0_gnn_b', 'L1_gnn_W1', 'L1_gnn_q1', 'L1_gnn_k1', 'L1_gnn_b1',
        'L1_gnn_W2', 'L1_gnn_q2', 'L1_gnn_k2', 'L1_gnn_b2']


def kernel(**inputs):
    import numpy as _np
    import concourse.bacc as _bacc
    from concourse import mybir as _mybir
    from concourse.bass_utils import run_bass_kernel_spmd as _run

    nc = _bacc.Bacc("TRN2", target_bir_lowering=False, num_devices=1)
    arrays, args = {}, []
    for name in _INS:
        a = _np.ascontiguousarray(inputs[name])
        arrays[f"in_{name}"] = a
        args.append(nc.dram_tensor(f"in_{name}", a.shape, _mybir.dt.from_np(a.dtype), kind="ExternalInput").ap())
    out = nc.dram_tensor("out_x", (N, D), F32, kind="ExternalOutput").ap()
    gnn_kernel(nc, *args, out)
    r = _run(nc, [arrays], core_ids=[0])
    return r.results[0]["out_x"]
```

```python
from contextlib import ExitStack

import concourse.bass as bass
from concourse import mybir

ALU = mybir.AluOpType
ACT = mybir.ActivationFunctionType
AX = mybir.AxisListType
F32 = mybir.dt.float32
BF16 = mybir.dt.bfloat16
F16 = mybir.dt.float16
I32 = mybir.dt.int32
ds = bass.ds

P = 128
N = 1250
E = 20000
D = 768
R = 3
NT = (N + P - 1) // P
NP_ = NT * P
KT = D // P
LAST = N - (NT - 1) * P
EP, EC = 125, 160
assert EP * EC == E
PAIR = 2 * P
MAXPAIRS = (E + NT * (PAIR - 1)) // PAIR
PAIRS_STEP = 3
NPAIR = R * NT * PAIRS_STEP
KB = 2 * PAIRS_STEP
SPREAD = 4
SPREAD_BANK = 2
MAX_AT = (1, 3, 5, 7, 8, 9)
MAX_STEPS = (R - 1) * len(MAX_AT)
SQ, SM = 32, 8
assert MAX_STEPS >= NT and len(MAX_AT) % 2 == 0
assert NPAIR >= MAXPAIRS + 2
T = 2 * NPAIR
HALF = D // 2
RING = 4
ROW = D + 4
GROUPS_W = {3: 2, 7: 2, 11: 1, 14: 1}
GROUPS_P = (2, 2, 2, 2, 1, 1, 1, 1, 1, 1)
ROUND = 12582912.0
NEG = -1.5e38
EPS_LN = 1e-5
EPS_Z = 1e-16
SLOPE = 0.2


def gnn_kernel(nc, x, src, dst, edge_type, W0, b0, W1, q1, k1, b1, W2, q2, k2, b2, out, debug=None):
    HEADS = {1: 4, 2: 1}
    Wd = {1: W1, 2: W2}
    qd = {1: q1, 2: q2}
    kd = {1: k1, 2: k2}
    bd = {0: b0, 1: b1, 2: b2}

    WIDTH = {0: D + 1, 1: D + HEADS[1], 2: D + HEADS[2]}
    rows = {l: nc.dram_tensor(f"rows{l}", [NP_ if l == 0 else R * NP_, WIDTH[l]], F32).ap() for l in (0, 1, 2)}
    keys = {l: nc.dram_tensor(f"keys{l}", [R * NP_, HEADS[l]], F32).ap() for l in (1, 2)}

    with ExitStack() as ctx:
        def sb(name, shape, dt=F32):
            return ctx.enter_context(nc.sbuf_tensor(name, shape, dt))

        def sem(name):
            return ctx.enter_context(nc.semaphore(name))

        ps = ctx.enter_context(nc.psum_tensor("ps", [P, 8, 512], F32))
        psf = ps[:, :, :].rearrange("p b c -> p (b c)")

        xs = sb("xs", [P, NT, D])
        hT = sb("hT", [P, KT, NP_])
        wreg = sb("wreg", [P, 2, KT, D])
        hw0 = wreg[:, :, :, :].rearrange("p a k d -> p (a k d)")[:, 0:NT * D].rearrange("p (t d) -> p t d", t=NT)
        stT = sb("stT", [P, (T + 2 * (SPREAD - 1)) * P], BF16)
        ring = sb("ring", [P, 2 * RING, ROW])
        ringf = ring[:, :, :].rearrange("p a d -> p (a d)")
        w0s = ringf[:, 0:KT * D].rearrange("p (k d) -> p k d", k=KT)
        hn = sb("hn", [P, 2, D])
        stage = sb("stage", [P, 2, ROW])
        zw = sb("zw", [P, 2, 2, 4, P])
        negm = hn[:, 0, 0:4 * P].rearrange("p (a b c) -> p a b c", a=2, b=2)
        s16 = sb("s16", [P, 2, P], BF16)
        bias = sb("bias", [P, D])
        etmp = sb("etmp", [P, D])
        qv = etmp[:, 0:NT * 2 * R * 4].rearrange("p (t q) -> p t q", t=NT)

        stf = stT[:, :].bitcast(F32)
        at = [0]

        def temp(words, dt=F32, parts=P):
            v = stf[0:parts, at[0]:at[0] + words]
            at[0] += words
            assert at[0] <= T * P // 2
            return v if dt == F32 else v.bitcast(dt)

        e_i = temp(3 * EC, I32, EP).rearrange("p (a c) -> p a c", a=3)
        e_f = temp(3 * EC, F32, EP).rearrange("p (a c) -> p a c", a=3)
        dtile = temp(EC, F32, EP)
        dloc = temp(EC, F32, EP)
        t_a = temp(EC, F32, EP)
        t_b = temp(EC, F32, EP)
        field1 = temp(EC, F32, EP)
        field2 = temp(EC, F32, EP)
        slot_hi = temp(EC, F32, EP)
        slot_lo = temp(EC, F32, EP)
        bucket = temp(NT * EC // 2, BF16, EP).rearrange("p (j c) -> p j c", j=NT)
        cumA = temp(NT * EC // 2, BF16, EP).rearrange("p (j c) -> p j c", j=NT)
        cumB = temp(NT * EC // 2, BF16, EP).rearrange("p (j c) -> p j c", j=NT)
        wpos = temp(NT * EC, F32, EP).rearrange("p (j c) -> p j c", j=NT)
        upper = temp(P, F32, EP)
        ones = temp(P, F32, EP)
        rowtot = temp(NT, F32, EP)
        PB = 8
        oh_lo = temp(PB * P // 2, F16, EP).rearrange("p (b c) -> p b c", b=PB)
        oh_tg = temp(PB * P // 2, F16, EP).rearrange("p (b c) -> p b c", b=PB)
        oh_hi = temp(PB * T, F16, EP).rearrange("p (b f c) -> p b f c", b=PB, f=2)
        dcol = temp(PB, F32, EP)
        wt = [temp(D) for _ in range(2)]

        iota_f = sb("iota_f", [P, T])
        iota_h = sb("iota_h", [P, T], F16)
        iota_p = sb("iota_p", [P, 1])
        ident = sb("ident", [P, P])
        ident16 = sb("ident16", [P, P], BF16)
        zero16 = sb("zero16", [P, 512], BF16)
        half = sb("half", [P, NT])
        wqk = {l: sb(f"wqk{l}", [P, KT, 2, R * HEADS[l]]) for l in (1, 2)}
        qk1 = sb("qk1", [P, KT, 2, HEADS[1]])
        qkb = zw[:, :, :, :, :].rearrange("p a b h c -> p (a b h c)")[:, 0:2 * D].rearrange("p (a d) -> p a d", a=2)
        al = sb("al", [P, T * 4])
        fields = al[:, 0:2 * T].rearrange("p (f c) -> p f c", f=2)
        t_r = al[:, 2 * T:3 * T]
        t_s = al[:, 3 * T:4 * T]
        tl = sb("tl", [P, T])
        idx0 = sb("idx0", [P, T], I32)
        idxr = sb("idxr", [P, T + KB], I32)
        idxs = sb("idxs", [P, 2 * RING], I32)
        kidx = sb("kidx", [P, 2, 2 * PAIRS_STEP], I32)
        rmask = sb("rmask", [P, T, R], BF16)
        tot = sb("tot", [P, NT])
        cnt = sb("cnt", [P, NT])
        pstart = sb("pstart", [P, 2, NT + 6])
        base = sb("base", [P, NT])
        bounds = sb("bounds", [P, NT + 1], I32)
        deg = sb("deg", [P, NT])
        dinv = sb("dinv", [P, NT])
        dinv2 = sb("dinv2", [P, NT])
        stats = sb("stats", [P, 2, 6])
        mv = sb("mv", [P, NT, 2])
        vare = sb("vare", [P, NT])
        rstd = sb("rstd", [P, NT])
        kst = sb("kst", [P, R, NT, 4])
        q16 = sb("q16", [P, NT, 3, R * 4], BF16)
        m16 = sb("m16", [P, NT, 3, 4], BF16)
        mx = sb("mx", [P, NT, 4])
        mxr = sb("mxr", [P, NT, 4])
        kb = sb("kb", [P, 2, 2 * PAIRS_STEP, 4])
        qs = etmp[:, 0:T * 4]
        me = qs
        atmp = sb("atmp", [P, KB * 4])
        btmp = sb("btmp", [P, KB * 4])
        ctmp = sb("ctmp", [P, KB * 4])
        z = sb("z", [P, 4])
        rz = sb("rz", [P, 4])
        qe = ringf[:, 0:T * R * 4]

        s_x = [sem(f"s_x{i}") for i in range(4)]
        s_edges = sem("s_edges")
        s_w0 = sem("s_w0")
        s_qk = sem("s_qk")
        s_qkb = sem("s_qkb")
        wq2_done = sem("wq2_done")
        ttr = sem("ttr")
        tg_in = sem("tg_in")
        dcol_in = sem("dcol_in")
        slots_f = sem("slots_f")
        s_bias = [sem(f"s_bias{i}") for i in range(3)]
        wprep_in = [sem("wprep_in0"), sem("wprep_in1")]
        consts = sem("consts")
        pool_c = sem("pool_c")
        xpad = sem("xpad")
        t_ready, t_free = sem("t_ready"), sem("t_free")
        wt_used = sem("wt_used")
        wq_copied = sem("wq_copied")
        ranks_in, ranks_out = sem("ranks_in"), sem("ranks_out")
        bounds_ready = sem("bounds_ready")
        perm_in, perm_free = sem("perm_in"), sem("perm_free")
        slots_ready = sem("slots_ready")
        var_ready, rstd_ready = sem("var_ready"), sem("rstd_ready")
        deg_ready, dinv_ready = sem("deg_ready"), sem("dinv_ready")
        hn_ready = sem("hn_ready")
        p_ready = sem("p_ready")
        hw_ready = sem("hw_ready")
        dve_c = sem("dve_c")
        s_rows0 = sem("s_rows0")
        g_sem = {l: [sem(f"g{l}_{i}") for i in range(2 * RING)] for l in (0, 1, 2)}
        g_in = {l: sem(f"g_in{l}") for l in (0, 1, 2)}
        w_in = {l: sem(f"w_in{l}") for l in (0, 1, 2)}
        w_used = {l: sem(f"w_used{l}") for l in (0, 1, 2)}
        ix = sem("ix")
        turn = sem("turn")
        o16_in = sem("o16_in")
        st_ready, st_copied = sem("st_ready"), sem("st_copied")
        acc_free = {l: sem(f"acc_free{l}") for l in (0, 1, 2)}
        x1_ready = sem("x1_ready")
        s_w = {l: sem(f"s_w{l}") for l in (1, 2)}
        s_wb = {l: [sem(f"s_wb{l}_{i}") for i in range(2)] for l in (1, 2)}
        stage_in = {l: sem(f"stage_in{l}") for l in (1, 2)}
        stage_out = {l: [sem(f"stage_out{l}_{i}") for i in range(2)] for l in (1, 2)}
        qv_done = sem("qv_done")
        kst_ready, s_keys = sem("kst_ready"), sem("s_keys")
        q16_ready = sem("q16_ready")
        st_tail = sem("st_tail")
        oh_in = sem("oh_in")
        spread_read = sem("spread_read")
        qe_done = {l: sem(f"qe_done{l}") for l in (1, 2)}
        qs_ready = sem("qs_ready")
        k_in = {l: [sem(f"k_in{l}_{i}") for i in range(2)] for l in (1, 2)}
        k_used = {l: sem(f"k_used{l}") for l in (1, 2)}
        k_ix = sem("k_ix")
        al_step = {l: sem(f"al_step{l}") for l in (1, 2)}
        nm_step = {l: sem(f"nm_step{l}") for l in (1, 2)}
        b_used = {l: sem(f"b_used{l}") for l in (1, 2)}
        m_chain = {l: sem(f"m_chain{l}") for l in (1, 2)}
        z_in = {l: sem(f"z_in{l}") for l in (1, 2)}
        z_done = {l: sem(f"z_done{l}") for l in (1, 2)}
        z_read = {l: sem(f"z_read{l}") for l in (1, 2)}
        m16_ready = sem("m16_ready")
        me_done = {l: sem(f"me_done{l}") for l in (1, 2)}
        al_ready, e_ready = sem("al_ready"), sem("e_ready")
        rz_ready, divided = sem("rz_ready"), sem("divided")
        elu_in, elu_neg, elu_exp = sem("elu_in"), sem("elu_neg"), sem("elu_exp")
        rows_go = {l: sem(f"rows_go{l}") for l in (1, 2)}
        o_ready = sem("o_ready")
        s_out = sem("s_out")
        s_dbg = sem("s_dbg")

        NW = R * KT
        tbank = [2 * (n % 2) for n in range(NW + NT)] + [4 + 2 * (n % 2) for n in range(2 * NT)]

        def tbuf(n):
            return psf[:, tbank[n] * 512:tbank[n] * 512 + D]

        def load_bounds(eng):
            eng.wait_ge(bounds_ready, 1)
            return [0] + [eng.value_load(bounds[0:1, j:j + 1], min_val=j, max_val=MAXPAIRS) for j in range(1, NT + 1)]

        locals_ = dict(locals())
        block = ctx.enter_context(nc.Block())

        @block.sync
        def _(sp):
            for a, v in enumerate((src, dst, edge_type)):
                sp.dma_start(e_i[:, a, :], v.rearrange("(p c) -> p c", p=EP)).then_inc(s_edges, 16)
            for n in range(3):
                sp.dma_start(xs[:, 3 * n:3 * n + 3, :],
                             x[3 * n * P:(3 * n + 3) * P, :].rearrange("(t p) d -> p t d", p=P)).then_inc(s_x[n], 16)
            sp.wait_ge(xpad, 1)
            sp.dma_start(xs[0:LAST, NT - 1, :], x[(NT - 1) * P:N, :]).then_inc(s_x[3], 16)
            for a, v in enumerate((qd[1], kd[1])):
                with nc.allow_non_contiguous_dma(reason="small vectors"):
                    sp.dma_start(qk1[:, :, a, :], v.rearrange("(t p) h -> p t h", p=P)).then_inc(s_qk, 16)
            def prepare_load(l, r, buf):
                sp.dma_start(wreg[:, buf, :, :], Wd[l][r].rearrange("(k p) n -> p k n", p=P)).then_inc(wprep_in[buf], 16)

            prepare_load(1, 0, 0)
            prepare_load(1, 1, 1)
            for a, v in enumerate((qd[2], kd[2])):
                sp.dma_start(qkb[:, a, :], v.rearrange("d o -> (d o)").partition_broadcast(P)).then_inc(s_qkb, 16)
            sp.dma_start(bias[:, :], bd[0].partition_broadcast(P)).then_inc(s_bias[0], 16)
            sp.wait_ge(wt_used, KT)
            prepare_load(1, 2, 0)
            sp.dma_start(w0s, W0.rearrange("(k p) n -> p k n", p=P)).then_inc(s_w0, 16)
            sp.wait_ge(wt_used, 2 * KT)
            prepare_load(2, 0, 1)
            for r in (1, 2):
                sp.wait_ge(wq2_done, r)
                prepare_load(2, r, 1)
            for nt in range(NT):
                sp.wait_ge(hw_ready, 2 * nt + 2)
                sp.dma_start(rows[0][nt * P:(nt + 1) * P, 0:D], hw0[:, nt, :]).then_inc(s_rows0, 16)
            sp.wait_ge(dinv_ready, 1)
            with nc.allow_non_contiguous_dma(reason="one column"):
                sp.dma_start(rows[0].rearrange("(t p) d -> p t d", p=P)[:, :, D:D + 1], dinv[:, :].unsqueeze(2)).then_inc(s_rows0, 16)
            bnd = load_bounds(sp)
            groups = (bnd[NT] + (RING - 1)) // RING

            def relay(l):
                sp.sem_inc(g_in[l], 1)
                with sp.Fori(0, groups) as g:
                    for s in range(2 * RING):
                        sp.wait_ge(g_sem[l][s], 16 * (g + 1))
                        sp.sem_inc(g_in[l], 1)

            relay(0)

            def load_weights(l, r):
                sp.dma_start(wreg[:, r % 2, :, :], Wd[l][r].rearrange("(k p) n -> p k n", p=P)).then_inc(s_wb[l][r % 2], 16)

            sp.wait_ge(x1_ready, NT)
            sp.dma_start(bias[:, :], bd[1].partition_broadcast(P)).then_inc(s_bias[1], 16)
            for l in (1, 2):
                if l == 1:
                    load_weights(1, 0)
                    load_weights(1, 1)
                for r in range(2):
                    sp.wait_ge(s_wb[l][r], 16)
                    sp.sem_inc(s_w[l], 1)
                sp.wait_ge(kst_ready, l)
                for r in range(R):
                    with nc.allow_non_contiguous_dma(reason="rows of keys"):
                        sp.dma_start(keys[l][r * NP_:(r + 1) * NP_, :].rearrange("(t p) h -> p t h", p=P),
                                     kst[:, r, :, 0:HEADS[l]]).then_inc(s_keys, 16)
                for r in range(R):
                    for nt in range(NT):
                        n = r * NT + nt
                        if n == NT + 1:
                            sp.wait_ge(p_ready, 2 * NT * (1 + R * (l - 1) + 1))
                            load_weights(l, 2)
                        if n == 2 * NT - 2:
                            sp.wait_ge(s_wb[l][0], 32)
                            sp.sem_inc(s_w[l], 1)
                        sp.wait_ge(stage_in[l], 4 + 2 * n + 2)
                        sp.dma_start(rows[l][r * NP_ + nt * P:r * NP_ + (nt + 1) * P, :], stage[:, nt % 2, 0:WIDTH[l]]).then_inc(stage_out[l][nt % 2], 16)
                if l == 1:
                    load_weights(2, 0)
                    load_weights(2, 1)
                relay(l)
                if l == 1:
                    sp.wait_ge(hn_ready, 3 * NT)
                    sp.dma_start(bias[:, :], bd[2].partition_broadcast(P)).then_inc(s_bias[2], 16)
            for j in range(NT):
                n = P if j < NT - 1 else LAST
                sp.wait_ge(o_ready, j + 1)
                sp.dma_start(out[j * P:j * P + n, :], xs[0:n, j, :]).then_inc(s_out, 16)
            sp.wait_ge(s_out, 16 * NT)
            if debug:
                pairs = debug(nc, locals_)
                for o, v in pairs:
                    sp.dma_start(o, v).then_inc(s_dbg, 16)
                sp.wait_ge(s_dbg, 16 * len(pairs))

        @block.gpsimd
        def _(pool):
            nc.gpsimd.iota(iota_f[:, :], [[1, T]], base=0, channel_multiplier=0, allow_small_or_imprecise_dtypes=True).then_inc(pool_c, 1)
            nc.gpsimd.iota(iota_h[:, :], [[1, T]], base=0, channel_multiplier=0, allow_small_or_imprecise_dtypes=True).then_inc(pool_c, 1)
            nc.gpsimd.iota(iota_p[:, :], [[0, 1]], base=0, channel_multiplier=1, allow_small_or_imprecise_dtypes=True).then_inc(pool_c, 1)
            nc.gpsimd.memset(half[:, :], -0.5).then_inc(pool_c, 1)
            nc.gpsimd.memset(zero16[:, :], 0.0).then_inc(pool_c, 1)
            nc.gpsimd.memset(ones[:, :], 1.0).then_inc(pool_c, 1)
            nc.gpsimd.memset(idxr[:, T:T + KB], 0).then_inc(pool_c, 1)
            pool.wait_ge(pool_c, 7)
            pool.wait_ge(var_ready, 1)
            nc.gpsimd.tensor_tensor(rstd[:, :], vare[:, :], half[:, :], ALU.pow).then_inc(rstd_ready, 1)
            pool.wait_ge(slots_f, 1)
            pool.sem_inc(tg_in, 1)
            with pool.Fori(0, EC // PB) as g:
                pool.wait_ge(tg_in, g * PB + 1)
                nc.gpsimd.tensor_copy(dcol[:, :], dloc[:, ds(g * PB, PB)]).then_inc(dcol_in, 1)
                pool.wait_ge(dcol_in, g + 1)
                pool.sem_inc(turn, 1)
                for b in range(PB):
                    pool.wait_ge(perm_free, g * PB + (b + 1))
                    pool.sem_inc(turn, 1)
                    nc.gpsimd.tensor_scalar(oh_tg[:, b, :], iota_h[0:EP, 0:P], dcol[:, b:b + 1], None, ALU.is_equal).then_inc(tg_in, 1)
            pool.wait_ge(deg_ready, 1)
            nc.gpsimd.tensor_tensor(dinv[:, :], deg[:, :], half[:, :], ALU.pow).then_inc(dinv_ready, 1)
            bnd = load_bounds(pool)
            groups = (bnd[NT] + (RING - 1)) // RING

            def gather_rows(l, idx, ix0):
                with pool.Fori(0, groups) as g:
                    pool.wait_ge(g_in[l], 2 * RING * g + 1)
                    nc.gpsimd.tensor_copy(idxs[:, :], idx[:, ds(g * (2 * RING), 2 * RING)]).then_inc(ix, 1)
                    pool.wait_ge(ix, g + (ix0 + 1))
                    pool.sem_inc(turn, 1)
                    for s in range(2 * RING):
                        if s % 2 == 0:
                            pool.wait_ge(w_used[l], g * (2 * RING) + (s + 2))
                            pool.sem_inc(turn, 1)
                        nc.gpsimd.indirect_dma_start(ring[:, s, 0:WIDTH[l]], None, rows[l], bass.IndirectOffsetOnAxis(idxs[:, s:s + 1], 0)).then_inc(g_sem[l][s], 16)

            pool.wait_ge(slots_ready, 1)
            pool.wait_ge(s_rows0, 16 * (NT + 1))
            gather_rows(0, idx0, 0)
            pool.wait_ge(var_ready, 2)
            nc.gpsimd.tensor_tensor(rstd[:, :], vare[:, :], half[:, :], ALU.pow).then_inc(rstd_ready, 1)
            ix_count = groups
            kix_count = 0
            for l in (1, 2):
                H = HEADS[l]
                batches2 = (bnd[NT] + (2 * PAIRS_STEP - 1)) // (2 * PAIRS_STEP)

                def ask_keys(hf, batch, n):
                    nc.gpsimd.tensor_copy(kidx[:, hf, :], idxr[:, ds(batch * KB, KB)]).then_inc(k_ix, 1)
                    pool.wait_ge(k_ix, n)
                    pool.sem_inc(turn, 1)
                    for s in range(KB):
                        nc.gpsimd.indirect_dma_start(kb[:, hf, s, 0:H], None, keys[l], bass.IndirectOffsetOnAxis(kidx[:, hf, s:s + 1], 0)).then_inc(k_in[l][hf], 16)

                def score(hf, g):
                    batch = 2 * g + hf
                    pool.wait_ge(k_in[l][hf], 16 * KB * g + 16 * KB)
                    nc.gpsimd.tensor_tensor(atmp[:, 0:KB * H].rearrange("p (c h) -> p c h", h=H), qs[:, ds(batch * (KB * H), KB * H)].rearrange("p (c h) -> p c h", h=H), kb[:, hf, :, 0:H], ALU.add).then_inc(k_used[l], 1)
                    pool.wait_ge(k_used[l], batch + 1)
                    pool.sem_inc(turn, 1)
                    nc.gpsimd.tensor_scalar(btmp[:, 0:KB * H], atmp[:, 0:KB * H], 0.0, SLOPE, ALU.min, ALU.mult).then_inc(b_used[l], 1)
                    nc.gpsimd.tensor_scalar(ctmp[:, 0:KB * H], atmp[:, 0:KB * H], 0.0, None, ALU.max).then_inc(b_used[l], 1)
                    pool.wait_ge(b_used[l], 2 * batch + 2)
                    nc.gpsimd.tensor_tensor(al[:, ds(batch * (KB * H), KB * H)], btmp[:, 0:KB * H], ctmp[:, 0:KB * H], ALU.add).then_inc(al_step[l], PAIRS_STEP)
                    pool.wait_ge(al_step[l], PAIRS_STEP * batch + PAIRS_STEP)

                pool.wait_ge(s_keys, 16 * R * l)
                ask_keys(0, 0, kix_count + 1)
                pool.wait_ge(qs_ready, l)
                with pool.Fori(0, batches2) as g:
                    ask_keys(1, 2 * g + 1, kix_count + (2 * g + 2))
                    score(0, g)
                    ask_keys(0, 2 * g + 2, kix_count + (2 * g + 3))
                    score(1, g)
                pool.wait_ge(k_in[l][0], 16 * KB * batches2 + 16 * KB)
                pool.sem_inc(turn, 1)
                kix_count = kix_count + (2 * batches2 + 1)
                for hf in range(2):
                    pool.wait_ge(stage_out[l][hf], 16 * R * NT // 2)
                pool.wait_ge(rows_go[l], 1)
                gather_rows(l, idxr, ix_count)
                ix_count = ix_count + groups

        @block.scalar
        def _(act):
            def copy_t(n, out_ap, func=ACT.Copy):
                act.wait_ge(t_ready, n + 1)
                return nc.scalar.activation(out_ap, tbuf(n), func)

            for n in range(NW):
                if n >= 2:
                    act.wait_ge(wt_used, n - 1)
                copy_t(n, wt[n % 2]).then_inc(t_free, 1)
            act.wait_ge(wt_used, NW)
            nc.scalar.activation(wqk[1][:, :, :, :], ps[:, 4, 0:KT * 2 * R * HEADS[1]].rearrange("p (k a q) -> p k a q", k=KT, a=2), ACT.Copy).then_inc(wq_copied, 1)
            for nt in range(NT):
                n = NW + nt
                copy_t(n, hT[:, :, nt * P:(nt + 1) * P], ACT.Relu).then_inc(t_free, 1)
                if nt >= 1:
                    for h in range(2):
                        act.wait_ge(p_ready, 2 * (nt - 1) + h + 1)
                        nc.scalar.activation(hw0[:, nt - 1, h * HALF:(h + 1) * HALF], ps[:, 4 + h, 0:HALF], ACT.Copy).then_inc(hw_ready, 1)
            for h in range(2):
                act.wait_ge(p_ready, 2 * (NT - 1) + h + 1)
                nc.scalar.activation(hw0[:, NT - 1, h * HALF:(h + 1) * HALF], ps[:, 4 + h, 0:HALF], ACT.Copy).then_inc(hw_ready, 1)
            bnd = load_bounds(act)
            act.wait_ge(perm_in, EC)
            for k in range(2 * (SPREAD - 1)):
                nc.scalar.activation(stT[:, ds(bnd[NT] * PAIR + k * P, P)], zero16[:, 0:P], ACT.Copy).then_inc(st_tail, 1)
            with act.Fori(0, bnd[NT]) as i:
                act.wait_ge(st_ready, i + 2)
                nc.scalar.activation(stT[:, ds(i * PAIR, PAIR)], ps[:, ds(i % 2 + 6, 1), 0:P].bitcast(BF16), ACT.Copy).then_inc(st_copied, 1)
            for l in (1, 2):
                H = HEADS[l]
                if l == 1:
                    for nt in range(NT):
                        copy_t(NW + NT + nt, hT[:, :, nt * P:(nt + 1) * P], ACT.Relu).then_inc(t_free, 1)
                for r in range(R):
                    for nt in range(NT):
                        b = nt % 2
                        if r * NT + nt >= 2:
                            act.wait_ge(stage_out[l][b], r * (16 * NT // 2) + 16 * (nt // 2))
                        for h in range(2):
                            act.wait_ge(p_ready, r * (2 * NT) + (2 * NT * (1 + R * (l - 1)) + 2 * nt + h + 1))
                            if H == 4:
                                o = stage[:, b, h * 2 * (HALF // 2 + 1):(h + 1) * 2 * (HALF // 2 + 1)].rearrange("p (a c) -> p a c", a=2)[:, :, 0:HALF // 2]
                                i_ = ps[:, 2 * b + h, 0:HALF].rearrange("p (a c) -> p a c", a=2)
                            else:
                                o = stage[:, b, h * HALF:(h + 1) * HALF]
                                i_ = ps[:, 2 * b + h, 0:HALF]
                            nc.scalar.activation(o, i_, ACT.Copy).then_inc(stage_in[l], 1)
                act.wait_ge(al_ready, l)
                nc.scalar.activation(al[:, 0:T * H], me[:, 0:T * H], ACT.Exp).then_inc(e_ready, 1)
                if l == 1:
                    W = HALF // 2 + 1
                    for j in range(NT):
                        act.wait_ge(rz_ready, j + 1)
                        act.wait_ge(t_ready, NW + 2 * NT + j - 1)
                        for h in range(4):
                            last = nc.scalar.activation(hn[:, j % 2, h * (D // 4):(h + 1) * (D // 4)], ps[:, 2 * (j % 2) + h // 2, (h % 2) * W:(h % 2) * W + D // 4], ACT.Copy, scale=rz[:, h:h + 1])
                        last.then_inc(divided, 1)
                        act.wait_ge(divided, j + 1)
                        act.sem_inc(acc_free[1], 1)
                        act.wait_ge(elu_in, j + 1)
                        if j >= 1:
                            act.wait_ge(hn_ready, 2 * NT + j)
                        nc.scalar.activation(etmp[:, :], hn[:, j % 2, :], ACT.Relu, scale=-1.0).then_inc(elu_neg, 1)
                        act.wait_ge(elu_neg, j + 1)
                        nc.scalar.activation(etmp[:, :], etmp[:, :], ACT.Exp, scale=-1.0).then_inc(elu_exp, 1)
                        if j >= 2:
                            copy_t(NW + 2 * NT + j - 2, hT[:, :, (j - 2) * P:(j - 1) * P]).then_inc(t_free, 1)
                    for j in (NT - 2, NT - 1):
                        copy_t(NW + 2 * NT + j, hT[:, :, j * P:(j + 1) * P]).then_inc(t_free, 1)

        @block.vector
        def _(dve):
            chain = [0]

            def link(ins):
                chain[0] += 1
                ins.then_inc(dve_c, 1)
                dve.wait_ge(dve_c, chain[0])

            V = nc.vector
            V.memset(xs[96:P, NT - 1, :], 0.0).then_inc(xpad, 1)
            dve.wait_ge(pool_c, 7)
            V.tensor_scalar(ident[:, :], iota_f[:, 0:P], iota_p[:, 0:1], None, ALU.is_equal).then_inc(consts, 1)
            V.tensor_scalar(ident16[:, :], iota_f[:, 0:P], iota_p[:, 0:1], None, ALU.is_equal).then_inc(consts, 1)
            V.tensor_scalar(upper[:, :], iota_f[0:EP, 0:P], iota_p[0:EP, 0:1], None, ALU.is_gt).then_inc(consts, 1)

            dve.wait_ge(s_edges, 48)
            link(V.tensor_copy(e_f, e_i))
            link(V.tensor_scalar(t_a, e_f[:, 1, :], 1.0 / P, -(P / 2 - 0.5) / P, ALU.mult, ALU.add))
            link(V.tensor_scalar(t_b, t_a, ROUND, None, ALU.add))
            link(V.tensor_scalar(dtile, t_b, -ROUND, None, ALU.add))
            link(V.scalar_tensor_tensor(dloc, dtile, -float(P), e_f[:, 1, :], ALU.mult, ALU.add))
            V.tensor_scalar(field1, e_f[:, 0, :], 1.0, None, ALU.add)
            link(V.tensor_scalar(t_a, dloc, 1.0, None, ALU.add))
            V.scalar_tensor_tensor(field2, e_f[:, 2, :], float(P), t_a, ALU.mult, ALU.add)
            for j in range(NT):
                last = V.tensor_scalar(bucket[:, j, :], dtile, float(j), None, ALU.is_equal)
            link(last)
            a, b, s = bucket, cumA, 1
            while s < EC:
                V.tensor_copy(b[:, :, 0:s], a[:, :, 0:s])
                link(V.tensor_tensor(b[:, :, s:EC], a[:, :, s:EC], a[:, :, 0:EC - s], ALU.add))
                a, b, s = b, (cumB if b is cumA else cumA), 2 * s
            cum = a
            V.tensor_copy(rowtot, cum[:, :, EC - 1]).then_inc(ranks_in, 1)
            dve.wait_ge(ranks_out, 1)
            link(V.tensor_scalar(cnt[:, :], ps[:, 7, NT:2 * NT], 1.0 / PAIR, (PAIR / 2 - 0.5) / PAIR, ALU.mult, ALU.add))
            link(V.tensor_scalar(tot[:, :], cnt[:, :], ROUND, None, ALU.add))
            V.memset(pstart[:, :, :], 0.0)
            link(V.tensor_scalar(cnt[:, :], tot[:, :], -ROUND, None, ALU.add))
            link(V.tensor_scalar(pstart[:, 0, 1:NT + 1], cnt[:, :], 1.0, None, ALU.max))
            u, s = 0, 1
            while s < NT:
                V.tensor_copy(pstart[:, 1 - u, 1:s + 1], pstart[:, u, 1:s + 1])
                link(V.tensor_tensor(pstart[:, 1 - u, s + 1:NT + 1], pstart[:, u, s + 1:NT + 1], pstart[:, u, 1:NT + 1 - s], ALU.add))
                u, s = 1 - u, 2 * s
            V.tensor_copy(bounds[:, :], pstart[:, u, 0:NT + 1]).then_inc(bounds_ready, 1)
            link(V.scalar_tensor_tensor(base[:, :], pstart[:, u, 0:NT], float(PAIR), ps[:, 7, 0:NT], ALU.mult, ALU.add))
            link(V.tensor_scalar(base[:, :], base[:, :], -1.0, None, ALU.add))
            link(V.tensor_tensor(wpos, cum, base[0:EP, :].unsqueeze(2).to_broadcast([EP, NT, EC]), ALU.add))
            link(V.tensor_tensor(wpos, wpos, bucket, ALU.mult))
            link(V.tensor_reduce(t_a, wpos.rearrange("p j c -> p c j"), AX.X, ALU.add))
            link(V.tensor_scalar(t_b, t_a, 1.0 / P, -(P / 2 - 0.5) / P, ALU.mult, ALU.add))
            link(V.tensor_scalar(t_b, t_b, ROUND, None, ALU.add))
            link(V.tensor_scalar(slot_hi, t_b, -ROUND, None, ALU.add))
            link(V.scalar_tensor_tensor(slot_lo, slot_hi, -float(P), t_a, ALU.mult, ALU.add))
            dve.sem_inc(slots_f, 1)
            def moments(j):
                V.bn_stats(stats[:, 0, :], xs[:, j, 0:HALF])
                link(V.bn_stats(stats[:, 1, :], xs[:, j, HALF:D]))
                link(V.bn_aggr(mv[:, j, :], stats[:, :, :].rearrange("p a c -> p (a c)")))

            for j in range(NT):
                if j % 3 == 0:
                    dve.wait_ge(s_x[j // 3], 16)
                if j == NT - 1:
                    dve.wait_ge(xpad, 1)
                moments(j)
            V.tensor_scalar(vare[:, :], mv[:, :, 1], EPS_LN, None, ALU.add).then_inc(var_ready, 1)
            dve.wait_ge(rstd_ready, 1)

            def edge_groups(first, count):
                with dve.Fori(first, first + count) as g:
                    for b in range(PB):
                        c = ds(g * PB + b, 1)
                        dve.wait_ge(perm_free, g * PB + (b + 1))
                        V.tensor_scalar(oh_lo[:, b, :], iota_h[0:EP, 0:P], slot_lo[:, c], None, ALU.is_equal)
                        V.tensor_scalar(oh_hi[:, b, 0, :], iota_h[0:EP, :], slot_hi[:, c], field1[:, c], ALU.is_equal, ALU.mult)
                        V.tensor_scalar(oh_hi[:, b, 1, :], iota_h[0:EP, :], slot_hi[:, c], field2[:, c], ALU.is_equal, ALU.mult).then_inc(perm_in, 1)

            def prepare(r):
                dve.wait_ge(wprep_in[1], 16 * (2 + r))
                if r == 0:
                    dve.wait_ge(s_qkb, 32)
                for k in range(KT):
                    for a in range(2):
                        n = (r * KT + k) * 2 + a
                        if n >= 2:
                            dve.wait_ge(ttr, n - 1)
                        V.tensor_tensor_reduce(stage[:, a, 0:D], wreg[:, 1, k, :], qkb[:, a, :], 1.0, 0.0, ALU.mult, ALU.add, wqk[2][:, k, a, r:r + 1]).then_inc(ttr, 1)
                dve.wait_ge(ttr, 2 * KT * (r + 1))
                dve.sem_inc(wq2_done, 1)

            sorted_ = sum(GROUPS_W.values())
            edge_groups(0, sorted_)
            for j in range(NT):
                if j >= 2:
                    dve.wait_ge(t_ready, NW + j - 1)
                V.tensor_scalar(hn[:, j % 2, :], xs[:, j, :], mv[:, j, 0:1], rstd[:, j:j + 1], ALU.subtract, ALU.mult).then_inc(hn_ready, 1)
                edge_groups(sorted_, GROUPS_P[j])
                sorted_ += GROUPS_P[j]
                if j < R:
                    prepare(j)
            V.memset(stage[:, :, :], 1.0)
            dve.wait_ge(perm_free, EC + PB)
            V.tensor_scalar(deg[:, :], ps[:, 7, 0:NT], 1.0, None, ALU.add).then_inc(deg_ready, 1)
            link(V.tensor_copy(fields[:, :, :], ps[:, 6, 0:2 * T].rearrange("p (f c) -> p f c", f=2)))
            link(V.tensor_scalar(t_s[:, :], fields[:, 0, :], -1.0, 0.0, ALU.add, ALU.max))
            V.tensor_copy(idx0[:, :], t_s[:, :])
            link(V.tensor_scalar(t_r[:, :], fields[:, 1, :], 1.0 / P, -(P / 2 + 0.5) / P, ALU.mult, ALU.add))
            link(V.tensor_scalar(t_r[:, :], t_r[:, :], ROUND, None, ALU.add))
            link(V.tensor_scalar(t_r[:, :], t_r[:, :], -ROUND, 0.0, ALU.add, ALU.max))
            link(V.scalar_tensor_tensor(tl[:, :], t_r[:, :], -float(P), fields[:, 1, :], ALU.mult, ALU.add))
            link(V.tensor_scalar(tl[:, :], tl[:, :], -1.0, None, ALU.add))
            for r in range(R):
                V.tensor_scalar(rmask[:, :, r], t_r[:, :], float(r), None, ALU.is_equal)
            link(V.scalar_tensor_tensor(t_s[:, :], t_r[:, :], float(NP_), t_s[:, :], ALU.mult, ALU.add))
            V.tensor_copy(idxr[:, 0:T], t_s[:, :]).then_inc(slots_ready, 1)
            dve.wait_ge(slots_ready, 1)
            bnd = load_bounds(dve)
            groups = (bnd[NT] + (RING - 1)) // RING
            batches2 = (bnd[NT] + (2 * PAIRS_STEP - 1)) // (2 * PAIRS_STEP)

            dve.wait_ge(dinv_ready, 1)
            dve.wait_ge(s_bias[0], 16)
            dve.wait_ge(hw_ready, 2 * NT)
            link(V.tensor_tensor(dinv2[:, :], dinv[:, :], dinv[:, :], ALU.mult))
            for j in range(NT):
                last = V.scalar_tensor_tensor(xs[:, j, :], hw0[:, j, :], dinv2[:, j:j + 1], xs[:, j, :], ALU.mult, ALU.add)
            link(last)
            for j in range(NT):
                last = V.tensor_tensor(xs[:, j, :], xs[:, j, :], bias[:, :], ALU.add)
            link(last)

            def finish0(j):
                dve.wait_ge(w_used[0], 2 * bnd[j + 1] + 2 * RING)
                x2 = xs[:, j, :].rearrange("p (a c) -> p a c", a=2)
                bk = 2 * (j % 2)
                link(V.scalar_tensor_tensor(x2, ps[:, bk:bk + 2, 0:HALF], dinv[:, j:j + 1], x2, ALU.mult, ALU.add))
                dve.sem_inc(acc_free[0], 1)
                dve.sem_inc(x1_ready, 1)
                moments(j)

            for j in range(NT):
                with dve.Fori(bnd[j], bnd[j + 1]) as i:
                    for b in range(2):
                        t = 2 * i + b
                        if b == 0:
                            dve.wait_ge(st_ready, i + 1)
                        V.tensor_scalar(s16[:, b, :], iota_h[:, 0:P], tl[:, ds(t, 1)], None, ALU.is_equal).then_inc(o16_in, 1)
                        dve.wait_ge(g_in[0], t + 2)
                        dve.wait_ge(w_used[0], t + (2 * RING - 1))
                        V.tensor_scalar(zw[:, 0, b, 0, :], iota_f[:, 0:P], tl[:, ds(t, 1)], ring[:, ds((i % RING) * 2 + b, 1), D:D + 1].rearrange("p a c -> p (a c)"), ALU.is_equal, ALU.mult).then_inc(w_in[0], 1)
                if j >= 1:
                    finish0(j - 1)
            finish0(NT - 1)
            V.tensor_scalar(vare[:, :], mv[:, :, 1], EPS_LN, None, ALU.add).then_inc(var_ready, 1)

            def spread_banks(width, stride):
                per = 512 // stride
                for a in range(-(-NPAIR // per)):
                    n = min(per, NPAIR - a * per)
                    c = (SPREAD_BANK + a) * 512
                    v = psf[:, c:c + n * stride].rearrange("p (i x) -> p i x", x=stride)[:, :, 0:2 * width]
                    yield 2 * a * per, 2 * n, v

            for l in (1, 2):
                H = HEADS[l]
                if l == 1:
                    dve.wait_ge(rstd_ready, 2)
                    for j in range(NT):
                        dve.wait_ge(t_ready, NW + NT + j - 1)
                        V.tensor_scalar(hn[:, j % 2, :], xs[:, j, :], mv[:, j, 0:1], rstd[:, j:j + 1], ALU.subtract, ALU.mult).then_inc(hn_ready, 1)
                if l == 2:
                    dve.wait_ge(s_keys, 16 * R)
                    for b in range(2):
                        dve.wait_ge(stage_out[1][b], 16 * R * NT // 2)
                    V.memset(stage[:, :, D:D + 1], 1.0)
                dve.wait_ge(qv_done, l)
                V.tensor_copy(kst[:, :, :, 0:H], ps[:, 0, 0:NT * 2 * R * H].rearrange("p (t a r h) -> p a r t h", t=NT, a=2, r=R)[:, 1]).then_inc(kst_ready, 1)
                link(V.tensor_copy(qv[:, :, 0:R * H], ps[:, 0, 0:NT * 2 * R * H].rearrange("p (t a q) -> p a t q", t=NT, a=2)[:, 0]))
                for part in range(3):
                    link(V.tensor_copy(q16[:, :, part, 0:R * H], qv[:, :, 0:R * H]))
                    if part < 2:
                        link(V.tensor_tensor(qv[:, :, 0:R * H], qv[:, :, 0:R * H], q16[:, :, part, 0:R * H], ALU.subtract))
                dve.sem_inc(q16_ready, 1)
                dve.wait_ge(g_in[l - 1], 2 * RING * groups + 1)
                dve.wait_ge(qe_done[l], 1)
                for t0, n, v in spread_banks(R * H, SQ):
                    for b in range(2):
                        last = V.tensor_tensor(qe[:, 0:T * R * H].rearrange("p (i b r h) -> p b i r h", b=2, r=R, h=H)[:, b, t0 // 2:(t0 + n) // 2],
                                               v.rearrange("p i (b r h) -> p b i r h", b=2, r=R)[:, b],
                                               rmask[:, :, :].rearrange("p (i b) r -> p b i r", b=2)[:, b, t0 // 2:(t0 + n) // 2].unsqueeze(3).to_broadcast([P, n // 2, R, H]), ALU.mult)
                link(last)
                dve.sem_inc(spread_read, 1)
                V.tensor_reduce(qs[:, 0:T * H].rearrange("p (t h) -> p t h", h=H), qe[:, 0:T * R * H].rearrange("p (t r h) -> p t h r", r=R, h=H), AX.X, ALU.add).then_inc(rows_go[l], 1)
                dve.wait_ge(rows_go[l], 1)
                dve.sem_inc(qs_ready, 1)

                if l == 2:
                    dve.wait_ge(s_bias[2], 16)
                    for j in range(NT):
                        last = V.tensor_tensor(xs[:, j, :], xs[:, j, :], bias[:, :], ALU.add)
                    link(last)
                def maxima(j):
                    bk = 4 + 2 * (j % 2)
                    dve.wait_ge(z_done[l], j + 1)
                    V.tensor_reduce(mx[:, j, 0:H], psf[:, bk * 512:bk * 512 + 2 * H * P].rearrange("p (b h e) -> p h b e", b=2, h=H), AX.XY, ALU.max).then_inc(z_read[l], 1)

                def mask(i, b):
                    V.tensor_scalar(negm[:, ds(i % 2, 1), b, :].rearrange("p a c -> p (a c)"), iota_f[:, 0:P], tl[:, ds(2 * i + b, 1)], NEG, ALU.not_equal, ALU.mult).then_inc(nm_step[l], 1)

                dve.sem_inc(m_chain[l], 1)
                for b in range(2):
                    V.tensor_scalar(negm[:, 0, b, :], iota_f[:, 0:P], tl[:, b:b + 1], NEG, ALU.not_equal, ALU.mult).then_inc(nm_step[l], 1)
                for j in range(NT):
                    run = zw[:, j % 2, :, 0:H, :]
                    if j >= 2:
                        dve.wait_ge(z_done[l], j - 1)
                    V.memset(run, 2 * NEG).then_inc(m_chain[l], 2)
                    with dve.Fori(bnd[j], bnd[j + 1]) as i:
                        dve.wait_ge(al_step[l], i + 1)
                        for b in range(2):
                            dve.wait_ge(nm_step[l], 2 * i + (b + 1))
                            dve.wait_ge(m_chain[l], 2 * i + (b + 1 + 2 * j + 2))
                            for h in range(H):
                                last = V.scalar_tensor_tensor(run[:, b, h, :], negm[:, ds(i % 2, 1), b, :].rearrange("p a c -> p (a c)"), al[:, ds((2 * i + b) * H + h, 1)], run[:, b, h, :], ALU.add, ALU.max)
                            last.then_inc(m_chain[l], 1)
                            mask(i + 1, b)
                    dve.wait_ge(m_chain[l], 2 * bnd[j + 1] + (2 * j + 3))
                    dve.sem_inc(z_in[l], 1)
                    if j >= 1:
                        maxima(j - 1)
                maxima(NT - 1)
                dve.sem_inc(z_in[l], MAX_STEPS - NT)
                dve.wait_ge(z_read[l], NT + 2)
                link(V.tensor_copy(mxr[:, :, 0:H], mx[:, :, 0:H]))
                for part in range(3):
                    link(V.tensor_copy(m16[:, :, part, 0:H], mxr[:, :, 0:H]))
                    if part < 2:
                        link(V.tensor_tensor(mxr[:, :, 0:H], mxr[:, :, 0:H], m16[:, :, part, 0:H], ALU.subtract))
                dve.wait_ge(al_step[l], 6 * batches2)
                dve.sem_inc(m16_ready, 1)
                dve.wait_ge(me_done[l], 1)
                for t0, n, v in spread_banks(H, SM):
                    last = V.tensor_tensor(me[:, t0 * H:(t0 + n) * H].rearrange("p (i x) -> p i x", x=2 * H), al[:, t0 * H:(t0 + n) * H].rearrange("p (i x) -> p i x", x=2 * H), v, ALU.subtract)
                link(last)
                dve.sem_inc(spread_read, 1)
                V.tensor_scalar(me[:, 0:T * H], me[:, 0:T * H], 0.0, None, ALU.min).then_inc(al_ready, 1)
                dve.wait_ge(e_ready, l)

                def sums(j):
                    dve.wait_ge(w_used[l], 2 * bnd[j + 1] + 2 * RING)
                    bk = 2 * (j % 2)
                    W = HALF // 2 + 1
                    if l == 1:
                        zs = ps[:, bk:bk + 2, 0:2 * W].rearrange("p a (b c) -> p a b c", b=2)[:, :, :, W - 1]
                        link(V.tensor_scalar(z[:, 0:4].rearrange("p (a b) -> p a b", a=2), zs, EPS_Z, None, ALU.add))
                    else:
                        link(V.tensor_scalar(z[:, 0:1], ps[:, bk + 1, HALF:HALF + 1], EPS_Z, None, ALU.add))
                    link(V.reciprocal(rz[:, 0:H], z[:, 0:H]))

                def add_bias(j):
                    if j == 0:
                        dve.wait_ge(s_bias[1], 16)
                    dve.wait_ge(divided, j + 1)
                    V.tensor_tensor(hn[:, j % 2, :], hn[:, j % 2, :], bias[:, :], ALU.add).then_inc(elu_in, 1)
                    dve.wait_ge(elu_in, j + 1)

                def elu(j):
                    dve.wait_ge(elu_exp, j + 1)
                    V.scalar_tensor_tensor(hn[:, j % 2, :], etmp[:, :], -1.0, hn[:, j % 2, :], ALU.add, ALU.max).then_inc(hn_ready, 1)

                def residual(j):
                    x2 = xs[:, j, :].rearrange("p (a c) -> p a c", a=2)
                    bk = 2 * (j % 2)
                    V.scalar_tensor_tensor(x2, ps[:, bk:bk + 2, 0:HALF], rz[:, 0:1], x2, ALU.mult, ALU.add).then_inc(o_ready, 1)
                    dve.wait_ge(o_ready, j + 1)
                    dve.sem_inc(acc_free[l], 1)

                dve.sem_inc(w_in[l], 1)
                for j in range(NT + 1):
                    if j < NT:
                        with dve.Fori(bnd[j], bnd[j + 1]) as i:
                            if H > 1:
                                dve.wait_ge(w_in[l], 2 * i + 1)
                                for b in range(2):
                                    V.tensor_scalar(zw[:, 1, b, 0, :], iota_f[:, 0:P], tl[:, ds(2 * i + b, 1)], None, ALU.is_equal).then_inc(oh_in, 1)
                            for b in range(2):
                                t = 2 * i + b
                                dve.wait_ge(w_used[l], t + (2 * RING - 1))
                                if H > 1:
                                    dve.wait_ge(oh_in, t + 1)
                                    last = V.tensor_tensor(zw[:, 0, b, :, :], zw[:, 1, b, 0:1, :].to_broadcast([P, H, P]), al[:, ds(t * H, H)].unsqueeze(2).to_broadcast([P, H, P]), ALU.mult)
                                else:
                                    last = V.tensor_scalar(zw[:, 0, b, 0, :], iota_f[:, 0:P], tl[:, ds(t, 1)], al[:, ds(t, 1)], ALU.is_equal, ALU.mult)
                                last.then_inc(w_in[l], 1)
                    if j >= 1:
                        sums(j - 1)
                        if l == 1:
                            dve.sem_inc(rz_ready, 1)
                            if j >= 2:
                                elu(j - 2)
                            add_bias(j - 1)
                        else:
                            residual(j - 1)
                if l == 1:
                    elu(NT - 1)

        @block.tensor
        def _(pe):
            mm = nc.tensor.matmul

            def transposes(n, tile):
                for k in range(KT):
                    last = nc.tensor.transpose(tbuf(n)[:, k * P:(k + 1) * P], tile(k), ident[:, :])
                last.then_inc(t_ready, 1)

            pe.wait_ge(consts, 3)
            pe.wait_ge(s_qk, 32)
            def wq_tile(n):
                r, k = n // KT, n % KT
                H = HEADS[1]
                pe.wait_ge(t_free, n + 1)
                o = ps[:, 4, 0:KT * 2 * R * H].rearrange("p (k a r h) -> p k a r h", k=KT, a=2, r=R)[:, k, :, r, :]
                for f in range(KT):
                    last = mm(o, wt[n % 2][:, f * P:(f + 1) * P], qk1[:, f, :, :], start=(f == 0), stop=(f == KT - 1))
                last.then_inc(wt_used, 1)

            def sort_group(g):
                c = PB * g
                if g == 0:
                    pe.wait_ge(perm_in, 1)
                    mm(ps[:, 6, 0:2 * T], zero16[0:EP, 0:P], zero16[0:EP, 0:2 * T], start=True, stop=False, skip_group_check=True)
                    mm(ps[:, 7, 0:NT], zero16[0:EP, 0:P], zero16[0:EP, 0:NT], start=True, stop=False, skip_group_check=True)
                for b in range(PB):
                    pe.wait_ge(perm_in, c + b + 1)
                    mm(ps[:, 6, 0:2 * T], oh_lo[:, b, :], oh_hi[:, b, :, :].rearrange("p f c -> p (f c)"), start=False, stop=False, skip_group_check=True)
                    pe.wait_ge(tg_in, c + b + 2)
                    mm(ps[:, 7, 0:NT], oh_tg[:, b, :], bucket[:, :, c + b], start=False, stop=False, skip_group_check=True).then_inc(perm_free, 1)

            sorted_ = 0
            for n in range(NW):
                r, k = n // KT, n % KT
                if n >= 2:
                    pe.wait_ge(t_free, n - 1)
                if k == 0:
                    pe.wait_ge(wprep_in[r % 2], 16 * (r // 2 + 1))
                transposes(n, lambda f: wreg[:, r % 2, k, f * P:(f + 1) * P])
                if n >= 1:
                    wq_tile(n - 1)
                if n == 1:
                    pe.wait_ge(ranks_in, 1)
                    mm(ps[:, 7, 0:NT], upper[:, :], rowtot, start=True, stop=True)
                    mm(ps[:, 7, NT:2 * NT], ones[:, :], rowtot, start=True, stop=True).then_inc(ranks_out, 1)
                    pe.sem_inc(perm_free, PB)
                for g in range(GROUPS_W.get(n, 0)):
                    sort_group(sorted_)
                    sorted_ += 1
            wq_tile(NW - 1)

            pe.wait_ge(s_w0, 16)
            pe.wait_ge(wq_copied, 1)
            for nt in range(NT):
                n = NW + nt
                pe.wait_ge(hn_ready, nt + 1)
                pe.wait_ge(t_free, n - 1)
                for k in range(KT):
                    last = nc.tensor.transpose(tbuf(n)[:, k * P:(k + 1) * P], hn[:, nt % 2, k * P:(k + 1) * P], ident[:, :])
                last.then_inc(t_ready, 1)
                for g in range(GROUPS_P[nt]):
                    sort_group(sorted_)
                    sorted_ += 1
                pe.wait_ge(t_free, n + 1)
                for h in range(2):
                    if nt >= 1:
                        pe.wait_ge(hw_ready, 2 * (nt - 1) + h + 1)
                    for k in range(KT):
                        last = mm(ps[:, 4 + h, 0:HALF], hT[:, k, nt * P:(nt + 1) * P], w0s[:, k, h * HALF:(h + 1) * HALF], start=(k == 0), stop=(k == KT - 1))
                    last.then_inc(p_ready, 1)
            assert sorted_ * PB == EC

            bnd = load_bounds(pe)

            def open_acc(l, j):
                if j >= 2:
                    pe.wait_ge(acc_free[l], j - 1)
                for a in range(2):
                    mm(ps[:, 2 * (j % 2) + a, 0:HALF + 2], zero16[:, 0:P], zero16[:, 0:HALF + 2], start=True, stop=False, skip_group_check=True)

            def spread(parts, width, stride, done):
                first = SPREAD_BANK * 512
                for a in range(-(-NPAIR * stride // 512)):
                    mm(psf[:, first + a * 512:first + (a + 1) * 512], zero16[:, 0:P], zero16[:, 0:512], start=True, stop=True)
                for j in range(NT):
                    with pe.Fori(bnd[j], bnd[j + 1], SPREAD) as i:
                        for k in range(2 * SPREAD):
                            for part in range(3):
                                mm(psf[:, ds(i * stride + (first + k // 2 * stride + k % 2 * width), width)], stT[:, ds(i * PAIR + k * P, P)], parts[:, j, part, 0:width], start=(part == 0), stop=(part == 2))
                mm(psf[:, first + NPAIR * stride:first + NPAIR * stride + 8], zero16[:, 0:P], zero16[:, 0:8], start=True, stop=True).then_inc(done, 1)

            pe.sem_inc(w_used[0], 2 * RING)
            pe.sem_inc(st_copied, 2)
            pe.sem_inc(st_ready, 1)
            for j in range(NT):
                open_acc(0, j)
                with pe.Fori(bnd[j], bnd[j + 1]) as i:
                    pe.wait_ge(o16_in, 2 * i + 2)
                    pe.wait_ge(st_copied, i + 1)
                    for b in range(2):
                        last = nc.tensor.transpose(ps[:, ds(i % 2 + 6, 1), 0:P].bitcast(BF16).rearrange("p o c -> p (o c)")[:, b * P:(b + 1) * P], s16[:, b, :], ident16[:, :])
                    last.then_inc(st_ready, 1)
                    for b in range(2):
                        pe.wait_ge(w_in[0], 2 * i + (b + 1))
                        for a in range(2):
                            last = mm(ps[:, 2 * (j % 2) + a, 0:HALF], zw[:, 0, b, 0, :], ring[:, ds((i % RING) * 2 + b, 1), a * HALF:(a + 1) * HALF].rearrange("p o c -> p (o c)"), start=False, stop=False, skip_group_check=True)
                        last.then_inc(w_used[0], 1)

            for l in (1, 2):
                H = HEADS[l]
                if l == 1:
                    pe.wait_ge(st_copied, bnd[NT] + 2)
                    for nt in range(NT):
                        n = NW + NT + nt
                        pe.wait_ge(hn_ready, NT + nt + 1)
                        pe.wait_ge(t_free, n - 1)
                        for k in range(KT):
                            last = nc.tensor.transpose(tbuf(n)[:, k * P:(k + 1) * P], hn[:, nt % 2, k * P:(k + 1) * P], ident[:, :])
                        last.then_inc(t_ready, 1)
                pe.wait_ge(t_free, NW + (l + 1) * NT)
                pe.wait_ge(acc_free[l - 1], NT)
                for nt in range(NT):
                    for k in range(KT):
                        last = mm(ps[:, 0, nt * 2 * R * H:(nt + 1) * 2 * R * H], hT[:, k, nt * P:(nt + 1) * P], wqk[l][:, k, :, :].rearrange("p a q -> p (a q)"), start=(k == 0), stop=(k == KT - 1))
                last.then_inc(qv_done, 1)
                pe.wait_ge(q16_ready, l)
                pe.wait_ge(st_tail, 2 * (SPREAD - 1))
                spread(q16, R * H, SQ, qe_done[l])
                pe.wait_ge(spread_read, 2 * l - 1)

                pe.sem_inc(z_read[l], 2)
                pe.sem_inc(stage_in[l], 4)

                def project(r, nt):
                    for h in range(2):
                        pe.wait_ge(stage_in[l], r * (2 * NT) + (2 * nt + h + 1))
                        for k in range(KT):
                            o = ds(r % 2, 1)
                            last = mm(ps[:, 2 * (nt % 2) + h, 0:HALF], hT[:, k, nt * P:(nt + 1) * P], wreg[:, o, k, h * HALF:(h + 1) * HALF].rearrange("p o c -> p (o c)"), start=(k == 0), stop=(k == KT - 1))
                        last.then_inc(p_ready, 1)

                pe.wait_ge(s_w[l], 1)
                for nt in range(NT):
                    project(0, nt)
                with pe.Fori(1, R) as r:
                    pe.wait_ge(s_w[l], r + 1)
                    for nt in range(NT):
                        project(r, nt)
                        if nt in MAX_AT:
                            m = MAX_AT.index(nt)
                            n = (r - 1) * len(MAX_AT) + m
                            pe.wait_ge(z_in[l], n + 1)
                            pe.wait_ge(z_read[l], n + 1)
                            for b in range(2):
                                for h in range(H):
                                    c = (4 + 2 * (m % 2)) * 512 + (b * H + h) * P
                                    last = nc.tensor.transpose(psf[:, c:c + P], zw[:, m % 2, b, h, :], ident[:, :])
                            last.then_inc(z_done[l], 1)
                pe.wait_ge(m16_ready, l)
                pe.wait_ge(stage_in[l], 4 + 2 * R * NT)
                spread(m16, H, SM, me_done[l])
                pe.wait_ge(spread_read, 2 * l)
                pe.sem_inc(w_used[l], 2 * RING)
                for j in range(NT + 1):
                    if j < NT:
                        open_acc(l, j)
                        with pe.Fori(bnd[j], bnd[j + 1]) as i:
                            for b in range(2):
                                pe.wait_ge(w_in[l], 2 * i + (b + 2))
                                pe.wait_ge(g_in[l], 2 * i + (b + 2))
                                row = ring[:, ds((i % RING) * 2 + b, 1), :].rearrange("p o c -> p (o c)")
                                W = HALF // 2 + 1
                                if H == 4:
                                    for h in range(H):
                                        last = mm(ps[:, 2 * (j % 2) + h // 2, (h % 2) * W:(h % 2 + 1) * W], zw[:, 0, b, h, :], row[:, h * W:(h + 1) * W], start=False, stop=False, skip_group_check=True)
                                else:
                                    mm(ps[:, 2 * (j % 2), 0:HALF], zw[:, 0, b, 0, :], row[:, 0:HALF], start=False, stop=False, skip_group_check=True)
                                    last = mm(ps[:, 2 * (j % 2) + 1, 0:HALF + 1], zw[:, 0, b, 0, :], row[:, HALF:D + 1], start=False, stop=False, skip_group_check=True)
                                last.then_inc(w_used[l], 1)
                    if l == 1 and j >= 3:
                        for nt in ([j - 3] if j < NT else [j - 3, j - 2, j - 1]):
                            n = NW + 2 * NT + nt
                            pe.wait_ge(hn_ready, 2 * NT + nt + 1)
                            pe.wait_ge(t_free, n - 1)
                            for k in range(KT):
                                last = nc.tensor.transpose(tbuf(n)[:, k * P:(k + 1) * P], hn[:, nt % 2, k * P:(k + 1) * P], ident[:, :])
                            last.then_inc(t_ready, 1)


_INS = ['x', 'src', 'dst', 'edge_type_3', 'L0_gnn_W', 'L0_gnn_b', 'L1_gnn_W1', 'L1_gnn_q1', 'L1_gnn_k1', 'L1_gnn_b1',
        'L1_gnn_W2', 'L1_gnn_q2', 'L1_gnn_k2', 'L1_gnn_b2']


def kernel(**inputs):
    import numpy as _np
    import concourse.bacc as _bacc
    from concourse import mybir as _mybir
    from concourse.bass_utils import run_bass_kernel_spmd as _run

    nc = _bacc.Bacc("TRN2", target_bir_lowering=False, num_devices=1)
    arrays, args = {}, []
    for name in _INS:
        a = _np.ascontiguousarray(inputs[name])
        arrays[f"in_{name}"] = a
        args.append(nc.dram_tensor(f"in_{name}", a.shape, _mybir.dt.from_np(a.dtype), kind="ExternalInput").ap())
    out = nc.dram_tensor("out_x", (N, D), F32, kind="ExternalOutput").ap()
    gnn_kernel(nc, *args, out)
    r = _run(nc, [arrays], core_ids=[0])
    return r.results[0]["out_x"]
```

```python
from contextlib import ExitStack

import concourse.bass as bass
from concourse import mybir

ALU = mybir.AluOpType
ACT = mybir.ActivationFunctionType
AX = mybir.AxisListType
F32 = mybir.dt.float32
BF16 = mybir.dt.bfloat16
F16 = mybir.dt.float16
I32 = mybir.dt.int32
ds = bass.ds

P = 128
N = 1250
E = 20000
D = 768
R = 3
NT = (N + P - 1) // P
NP_ = NT * P
KT = D // P
LAST = N - (NT - 1) * P
EP, EC = 125, 160
assert EP * EC == E
PAIR = 2 * P
MAXPAIRS = (E + NT * (PAIR - 1)) // PAIR
PAIRS_STEP = 3
NPAIR = R * NT * PAIRS_STEP
KB = 2 * PAIRS_STEP
SPREAD = 6
BANK_Q, BANK_M = 2, 6
MAX_AT = {11: (0,), 14: (1,), 17: (2,), 19: (3,), 21: (4,), 23: (5,), 25: (6,), 27: (7,), 28: (8,), 29: (9, 10, 11)}
SQ, SM = 32, 8
assert max(MAX_AT) == R * NT - 1 and min(MAX_AT) >= NT
assert NPAIR >= MAXPAIRS + 2 and 6 * R <= SQ and 6 <= SM
T = 2 * NPAIR
HALF = D // 2
RING = 4
ROW = D + 4
PB = 8
GROUP_AFTER = (3, 5, 7, 9, 10, 12, 13, 15, 16, 17)
assert (len(GROUP_AFTER) + NT) * PB == EC
BIAS_AT = {3: (0, 1), 4: (2, 3), 5: (4,), 6: (5,), 7: (6,), 8: (7,), 9: (8, 9)}
ROUND = 12582912.0
NEG = -1.5e38
EPS_LN = 1e-5
EPS_Z = 1e-16
SLOPE = 0.2


def gnn_kernel(nc, x, src, dst, edge_type, W0, b0, W1, q1, k1, b1, W2, q2, k2, b2, out):
    HEADS = {1: 4, 2: 1}
    Wd = {1: W1, 2: W2}
    qd = {1: q1, 2: q2}
    kd = {1: k1, 2: k2}
    bd = {0: b0, 1: b1, 2: b2}

    WIDTH = {0: D + 1, 1: D + HEADS[1], 2: D + HEADS[2]}
    rows = {l: nc.dram_tensor(f"rows{l}", [NP_ if l == 0 else R * NP_, WIDTH[l]], F32).ap() for l in (0, 1, 2)}
    keys = {l: nc.dram_tensor(f"keys{l}", [R * NP_, HEADS[l]], F32).ap() for l in (1, 2)}

    with ExitStack() as ctx:
        def sb(name, shape, dt=F32):
            return ctx.enter_context(nc.sbuf_tensor(name, shape, dt))

        def sem(name):
            return ctx.enter_context(nc.semaphore(name))

        ps = ctx.enter_context(nc.psum_tensor("ps", [P, 8, 512], F32))
        psf = ps[:, :, :].rearrange("p b c -> p (b c)")

        xs = sb("xs", [P, NT, D])
        hT = sb("hT", [P, KT, NP_])
        wreg = sb("wreg", [P, 2, KT, D])
        hw0 = wreg[:, :, :, :].rearrange("p a k d -> p (a k d)")[:, 0:NT * D].rearrange("p (t d) -> p t d", t=NT)
        stT = sb("stT", [P, (T + 2 * (SPREAD - 1)) * P], BF16)
        ring = sb("ring", [P, 2 * RING, ROW])
        ringf = ring[:, :, :].rearrange("p a d -> p (a d)")
        w0s = ringf[:, 0:KT * D].rearrange("p (k d) -> p k d", k=KT)
        hn = sb("hn", [P, 2, D])
        stage = sb("stage", [P, 2, ROW])
        zw = sb("zw", [P, 2, 2, 4, P])
        negm = hn[:, 0, 0:4 * P].rearrange("p (a b c) -> p a b c", a=2, b=2)
        scored = hn[:, :, :].rearrange("p a d -> p (a d)")[:, 4 * P:12 * P].rearrange("p (b h c) -> p b h c", b=2, h=4)
        s16 = sb("s16", [P, 2, P], BF16)
        bias = sb("bias", [P, D])
        etmp = sb("etmp", [P, D])
        qv = etmp[:, 0:NT * 2 * R * 4].rearrange("p (t q) -> p t q", t=NT)

        stf = stT[:, :].bitcast(F32)
        at = [0]

        def temp(words, dt=F32, parts=P):
            v = stf[0:parts, at[0]:at[0] + words]
            at[0] += words
            assert at[0] <= T * P // 2
            return v if dt == F32 else v.bitcast(dt)

        e_i = temp(3 * EC, I32, EP).rearrange("p (a c) -> p a c", a=3)
        e_f = temp(3 * EC, F32, EP).rearrange("p (a c) -> p a c", a=3)
        dtile = temp(EC, F32, EP)
        dloc = temp(EC, F32, EP)
        t_a = temp(EC, F32, EP)
        t_b = temp(EC, F32, EP)
        field1 = temp(EC, F32, EP)
        field2 = temp(EC, F32, EP)
        slot_hi = temp(EC, F32, EP)
        slot_lo = temp(EC, F32, EP)
        bucket = temp(NT * EC // 2, BF16, EP).rearrange("p (j c) -> p j c", j=NT)
        cumA = temp(NT * EC // 2, BF16, EP).rearrange("p (j c) -> p j c", j=NT)
        cumB = temp(NT * EC // 2, BF16, EP).rearrange("p (j c) -> p j c", j=NT)
        wpos = temp(NT * EC, F32, EP).rearrange("p (j c) -> p j c", j=NT)
        upper = temp(P, F32, EP)
        ones = temp(P, F32, EP)
        rowtot = temp(NT, F32, EP)
        oh_lo = temp(PB * P // 2, F16, EP).rearrange("p (b c) -> p b c", b=PB)
        oh_tg = temp(PB * P // 2, F16, EP).rearrange("p (b c) -> p b c", b=PB)
        oh_hi = temp(PB * T, F16, EP).rearrange("p (b f c) -> p b f c", b=PB, f=2)
        dcol = temp(PB, F32, EP)
        wt = [temp(D) for _ in range(2)]

        iota_f = sb("iota_f", [P, T])
        iota_h = sb("iota_h", [P, T], F16)
        iota_p = sb("iota_p", [P, 1])
        ident = sb("ident", [P, P])
        ident16 = sb("ident16", [P, P], BF16)
        zero16 = sb("zero16", [P, 512], BF16)
        half = sb("half", [P, NT])
        wqk = {l: sb(f"wqk{l}", [P, KT, 2, R * HEADS[l]]) for l in (1, 2)}
        qk1 = sb("qk1", [P, KT, 2, HEADS[1]])
        qkb = zw[:, :, :, :, :].rearrange("p a b h c -> p (a b h c)")[:, 0:2 * D].rearrange("p (a d) -> p a d", a=2)
        al = sb("al", [P, T * 4])
        fields = al[:, 0:2 * T].rearrange("p (f c) -> p f c", f=2)
        t_r = al[:, 2 * T:3 * T]
        t_s = al[:, 3 * T:4 * T]
        tl = sb("tl", [P, T])
        idx0 = sb("idx0", [P, T], I32)
        idxr = sb("idxr", [P, T + KB], I32)
        idxs = sb("idxs", [P, 2 * RING], I32)
        kidx = sb("kidx", [P, 2, 2 * PAIRS_STEP], I32)
        rmask = sb("rmask", [P, T, R], BF16)
        tot = sb("tot", [P, NT])
        cnt = sb("cnt", [P, NT])
        pstart = sb("pstart", [P, 2, NT + 6])
        base = sb("base", [P, NT])
        bounds = sb("bounds", [P, NT + 1], I32)
        deg = sb("deg", [P, NT])
        dinv = sb("dinv", [P, NT])
        dinv2 = sb("dinv2", [P, NT])
        stats = sb("stats", [P, 2, 6])
        mv = sb("mv", [P, NT, 2])
        vare = sb("vare", [P, NT])
        rstd = sb("rstd", [P, NT])
        kst = sb("kst", [P, R, NT, 4])
        q16 = sb("q16", [P, NT, 3, R * 4], BF16)
        m16 = sb("m16", [P, NT, 3, 4], BF16)
        mx = sb("mx", [P, NT, 4])
        kb = sb("kb", [P, 2, 2 * PAIRS_STEP, 4])
        qs = etmp[:, 0:T * 4]
        me = qs
        atmp = sb("atmp", [P, 2, KB * 4])
        btmp = sb("btmp", [P, 2, KB * 4])
        ctmp = sb("ctmp", [P, 2, KB * 4])
        z = sb("z", [P, 4])
        rz = sb("rz", [P, 4])
        qe = ringf[:, 0:T * R * 4]

        s_x = [sem(f"s_x{i}") for i in range(4)]
        s_edges = sem("s_edges")
        s_w0 = sem("s_w0")
        s_qk = sem("s_qk")
        s_qkb = sem("s_qkb")
        wq2_done = sem("wq2_done")
        ttr = sem("ttr")
        tg_in = sem("tg_in")
        dcol_in = sem("dcol_in")
        slots_f = sem("slots_f")
        s_bias = [sem(f"s_bias{i}") for i in range(3)]
        wprep_in = [sem("wprep_in0"), sem("wprep_in1")]
        consts = sem("consts")
        pool_c = sem("pool_c")
        xpad = sem("xpad")
        t_ready, t_free = sem("t_ready"), sem("t_free")
        wt_used = sem("wt_used")
        wq_copied = sem("wq_copied")
        ranks_in, ranks_out = sem("ranks_in"), sem("ranks_out")
        bounds_ready = sem("bounds_ready")
        perm_in, perm_free = sem("perm_in"), sem("perm_free")
        slots_ready = sem("slots_ready")
        var_ready, rstd_ready = sem("var_ready"), sem("rstd_ready")
        deg_ready, dinv_ready = sem("deg_ready"), sem("dinv_ready")
        hn_ready = sem("hn_ready")
        p_ready = sem("p_ready")
        hw_ready = sem("hw_ready")
        dve_c = sem("dve_c")
        s_rows0 = sem("s_rows0")
        g_sem = {l: [sem(f"g{l}_{i}") for i in range(2 * RING)] for l in (0, 1, 2)}
        g_in = {l: sem(f"g_in{l}") for l in (0, 1, 2)}
        w_in = {l: sem(f"w_in{l}") for l in (0, 1, 2)}
        w_used = {l: sem(f"w_used{l}") for l in (0, 1, 2)}
        ix = sem("ix")
        turn = sem("turn")
        o16_in = sem("o16_in")
        st_ready, st_copied = sem("st_ready"), sem("st_copied")
        acc_free = {l: sem(f"acc_free{l}") for l in (0, 1, 2)}
        x1_ready = sem("x1_ready")
        s_w = {l: sem(f"s_w{l}") for l in (1, 2)}
        s_wb = {l: [sem(f"s_wb{l}_{i}") for i in range(2)] for l in (1, 2)}
        stage_in = {l: sem(f"stage_in{l}") for l in (1, 2)}
        stage_out = {l: [sem(f"stage_out{l}_{i}") for i in range(2)] for l in (1, 2)}
        qv_done = sem("qv_done")
        kst_ready, s_keys = sem("kst_ready"), sem("s_keys")
        q16_ready = sem("q16_ready")
        st_tail = sem("st_tail")
        onehot_in = sem("onehot_in")
        spread_read = sem("spread_read")
        q_spread = {l: sem(f"q_spread{l}") for l in (1, 2)}
        qs_ready = sem("qs_ready")
        k_in = {l: [sem(f"k_in{l}_{i}") for i in range(2)] for l in (1, 2)}
        k_used = {l: sem(f"k_used{l}") for l in (1, 2)}
        k_ix = sem("k_ix")
        al_step = {l: sem(f"al_step{l}") for l in (1, 2)}
        nm_step = {l: sem(f"nm_step{l}") for l in (1, 2)}
        b_used = {l: sem(f"b_used{l}") for l in (1, 2)}
        m_chain = {l: sem(f"m_chain{l}") for l in (1, 2)}
        z_in = {l: sem(f"z_in{l}") for l in (1, 2)}
        z_done = {l: sem(f"z_done{l}") for l in (1, 2)}
        z_read = {l: sem(f"z_read{l}") for l in (1, 2)}
        m16_ready = sem("m16_ready")
        m_spread = {l: sem(f"m_spread{l}") for l in (1, 2)}
        al_ready, e_ready = sem("al_ready"), sem("e_ready")
        rz_ready, divided = sem("rz_ready"), sem("divided")
        elu_in, elu_neg, elu_exp = sem("elu_in"), sem("elu_neg"), sem("elu_exp")
        rows_go = {l: sem(f"rows_go{l}") for l in (1, 2)}
        o_ready = sem("o_ready")
        s_out = sem("s_out")

        NW = R * KT
        tbank = [2 * (n % 2) for n in range(NW + NT)] + [4 + 2 * (n % 2) for n in range(2 * NT)]

        def tbuf(n):
            return psf[:, tbank[n] * 512:tbank[n] * 512 + D]

        def load_bounds(eng):
            eng.wait_ge(bounds_ready, 1)
            return [0] + [eng.value_load(bounds[0:1, j:j + 1], min_val=j, max_val=MAXPAIRS) for j in range(1, NT + 1)]

        block = ctx.enter_context(nc.Block())

        @block.sync
        def _(sp):
            for a, v in enumerate((src, dst, edge_type)):
                sp.dma_start(e_i[:, a, :], v.rearrange("(p c) -> p c", p=EP)).then_inc(s_edges, 16)
            for n in range(3):
                sp.dma_start(xs[:, 3 * n:3 * n + 3, :],
                             x[3 * n * P:(3 * n + 3) * P, :].rearrange("(t p) d -> p t d", p=P)).then_inc(s_x[n], 16)
            sp.wait_ge(xpad, 1)
            sp.dma_start(xs[0:LAST, NT - 1, :], x[(NT - 1) * P:N, :]).then_inc(s_x[3], 16)
            for a, v in enumerate((qd[1], kd[1])):
                with nc.allow_non_contiguous_dma(reason="small vectors"):
                    sp.dma_start(qk1[:, :, a, :], v.rearrange("(t p) h -> p t h", p=P)).then_inc(s_qk, 16)
            def prepare_load(l, r, buf):
                sp.dma_start(wreg[:, buf, :, :], Wd[l][r].rearrange("(k p) n -> p k n", p=P)).then_inc(wprep_in[buf], 16)

            prepare_load(1, 0, 0)
            prepare_load(1, 1, 1)
            for a, v in enumerate((qd[2], kd[2])):
                sp.dma_start(qkb[:, a, :], v.rearrange("d o -> (d o)").partition_broadcast(P)).then_inc(s_qkb, 16)
            sp.dma_start(bias[:, :], bd[0].partition_broadcast(P)).then_inc(s_bias[0], 16)
            sp.wait_ge(wt_used, KT)
            prepare_load(1, 2, 0)
            sp.dma_start(w0s, W0.rearrange("(k p) n -> p k n", p=P)).then_inc(s_w0, 16)
            sp.wait_ge(wt_used, 2 * KT)
            prepare_load(2, 0, 1)
            for r in (1, 2):
                sp.wait_ge(wq2_done, r)
                prepare_load(2, r, 1)
            bnd = load_bounds(sp)
            for nt in range(NT):
                if nt == NT - 1:
                    sp.wait_ge(dinv_ready, 1)
                    with nc.allow_non_contiguous_dma(reason="one column"):
                        sp.dma_start(rows[0].rearrange("(t p) d -> p t d", p=P)[:, :, D:D + 1], dinv[:, :].unsqueeze(2)).then_inc(s_rows0, 16)
                sp.wait_ge(hw_ready, 2 * nt + 2)
                sp.dma_start(rows[0][nt * P:(nt + 1) * P, 0:D], hw0[:, nt, :]).then_inc(s_rows0, 16)
            groups = (bnd[NT] + (RING - 1)) // RING

            def relay(l):
                sp.sem_inc(g_in[l], RING + 1)
                with sp.Fori(0, groups) as g:
                    for s in range(2 * RING):
                        sp.wait_ge(g_sem[l][s], 16 * (g + 1))
                        sp.sem_inc(g_in[l], 1)

            relay(0)

            def load_weights(l, r):
                sp.dma_start(wreg[:, r % 2, :, :], Wd[l][r].rearrange("(k p) n -> p k n", p=P)).then_inc(s_wb[l][r % 2], 16)

            sp.wait_ge(x1_ready, NT)
            sp.dma_start(bias[:, :], bd[1].partition_broadcast(P)).then_inc(s_bias[1], 16)
            for l in (1, 2):
                if l == 1:
                    load_weights(1, 0)
                    load_weights(1, 1)
                for r in range(2):
                    sp.wait_ge(s_wb[l][r], 16)
                    sp.sem_inc(s_w[l], 1)
                sp.wait_ge(kst_ready, 2 * l)
                for r in range(R):
                    with nc.allow_non_contiguous_dma(reason="rows of keys"):
                        sp.dma_start(keys[l][r * NP_:(r + 1) * NP_, :].rearrange("(t p) h -> p t h", p=P),
                                     kst[:, r, :, 0:HEADS[l]]).then_inc(s_keys, 16)
                for r in range(R):
                    for nt in range(NT):
                        n = r * NT + nt
                        if n == NT + 1:
                            sp.wait_ge(p_ready, 2 * NT * (1 + R * (l - 1) + 1))
                            load_weights(l, 2)
                        if n == 2 * NT - 2:
                            sp.wait_ge(s_wb[l][0], 32)
                            sp.sem_inc(s_w[l], 1)
                        sp.wait_ge(stage_in[l], 4 + 2 * n + 2)
                        sp.dma_start(rows[l][r * NP_ + nt * P:r * NP_ + (nt + 1) * P, :], stage[:, nt % 2, 0:WIDTH[l]]).then_inc(stage_out[l][nt % 2], 16)
                relay(l)
                if l == 1:
                    load_weights(2, 0)
                    load_weights(2, 1)
                    sp.wait_ge(hn_ready, 3 * NT)
                    sp.dma_start(bias[:, :], bd[2].partition_broadcast(P)).then_inc(s_bias[2], 16)
            for j in range(NT):
                n = P if j < NT - 1 else LAST
                sp.wait_ge(o_ready, j + 1)
                sp.dma_start(out[j * P:j * P + n, :], xs[0:n, j, :]).then_inc(s_out, 16)
            sp.wait_ge(s_out, 16 * NT)

        @block.gpsimd
        def _(pool):
            nc.gpsimd.iota(iota_f[:, :], [[1, T]], base=0, channel_multiplier=0, allow_small_or_imprecise_dtypes=True).then_inc(pool_c, 1)
            nc.gpsimd.iota(iota_h[:, :], [[1, T]], base=0, channel_multiplier=0, allow_small_or_imprecise_dtypes=True).then_inc(pool_c, 1)
            nc.gpsimd.iota(iota_p[:, :], [[0, 1]], base=0, channel_multiplier=1, allow_small_or_imprecise_dtypes=True).then_inc(pool_c, 1)
            nc.gpsimd.memset(half[:, :], -0.5).then_inc(pool_c, 1)
            nc.gpsimd.memset(zero16[:, :], 0.0).then_inc(pool_c, 1)
            nc.gpsimd.memset(ones[:, :], 1.0).then_inc(pool_c, 1)
            nc.gpsimd.memset(idxr[:, T:T + KB], 0).then_inc(pool_c, 1)
            pool.wait_ge(pool_c, 7)
            bnd = load_bounds(pool)
            pool.wait_ge(var_ready, 1)
            nc.gpsimd.tensor_tensor(rstd[:, :], vare[:, :], half[:, :], ALU.pow).then_inc(rstd_ready, 1)
            pool.wait_ge(slots_f, 1)
            pool.sem_inc(tg_in, 1)
            with pool.Fori(0, EC // PB) as g:
                pool.wait_ge(tg_in, g * PB + 1)
                nc.gpsimd.tensor_copy(dcol[:, :], dloc[:, ds(g * PB, PB)]).then_inc(dcol_in, 1)
                pool.wait_ge(dcol_in, g + 1)
                pool.sem_inc(turn, 1)
                for b in range(PB):
                    pool.wait_ge(perm_free, g * PB + (b + 1))
                    pool.sem_inc(turn, 1)
                    nc.gpsimd.tensor_scalar(oh_tg[:, b, :], iota_h[0:EP, 0:P], dcol[:, b:b + 1], None, ALU.is_equal).then_inc(tg_in, 1)
            pool.wait_ge(deg_ready, 1)
            nc.gpsimd.tensor_tensor(dinv[:, :], deg[:, :], half[:, :], ALU.pow).then_inc(dinv_ready, 1)
            groups = (bnd[NT] + (RING - 1)) // RING

            def gather_rows(l, idx, ix0):
                with pool.Fori(0, groups) as g:
                    for side in range(2):
                        pool.wait_ge(g_in[l], 2 * RING * g + (RING * side + 1))
                        nc.gpsimd.tensor_copy(idxs[:, RING * side:RING * (side + 1)], idx[:, ds(g * (2 * RING) + RING * side, RING)]).then_inc(ix, 1)
                        pool.wait_ge(ix, 2 * g + (ix0 + side + 1))
                        pool.sem_inc(turn, 1)
                        for s in range(RING * side, RING * (side + 1)):
                            if s % 2 == 0:
                                pool.wait_ge(w_used[l], g * (2 * RING) + (s + 2))
                                pool.sem_inc(turn, 1)
                            nc.gpsimd.indirect_dma_start(ring[:, s, 0:WIDTH[l]], None, rows[l], bass.IndirectOffsetOnAxis(idxs[:, s:s + 1], 0)).then_inc(g_sem[l][s], 16)

            pool.wait_ge(slots_ready, 1)
            pool.wait_ge(s_rows0, 16 * (NT + 1))
            gather_rows(0, idx0, 0)
            pool.wait_ge(var_ready, 2)
            nc.gpsimd.tensor_tensor(rstd[:, :], vare[:, :], half[:, :], ALU.pow).then_inc(rstd_ready, 1)
            ix_count = 2 * groups
            kix_count = 0
            for l in (1, 2):
                H = HEADS[l]
                batches2 = (bnd[NT] + (2 * PAIRS_STEP - 1)) // (2 * PAIRS_STEP)

                def ask_keys(side, batch, n):
                    nc.gpsimd.tensor_copy(kidx[:, side, :], idxr[:, ds(batch * KB, KB)]).then_inc(k_ix, 1)
                    pool.wait_ge(k_ix, n)
                    pool.sem_inc(turn, 1)
                    for s in range(KB):
                        nc.gpsimd.indirect_dma_start(kb[:, side, s, 0:H], None, keys[l], bass.IndirectOffsetOnAxis(kidx[:, side, s:s + 1], 0)).then_inc(k_in[l][side], 16)

                def score(side, g):
                    batch = 2 * g + side
                    pool.wait_ge(k_in[l][side], 16 * KB * g + 16 * KB)
                    nc.gpsimd.tensor_tensor(atmp[:, side, 0:KB * H].rearrange("p (c h) -> p c h", h=H), qs[:, ds(batch * (KB * H), KB * H)].rearrange("p (c h) -> p c h", h=H), kb[:, side, :, 0:H], ALU.add).then_inc(k_used[l], 1)
                    pool.wait_ge(k_used[l], batch + 1)
                    pool.sem_inc(turn, 1)
                    nc.gpsimd.tensor_scalar(btmp[:, side, 0:KB * H], atmp[:, side, 0:KB * H], 0.0, SLOPE, ALU.min, ALU.mult).then_inc(b_used[l], 1)
                    nc.gpsimd.tensor_scalar(ctmp[:, side, 0:KB * H], atmp[:, side, 0:KB * H], 0.0, None, ALU.max).then_inc(b_used[l], 1)
                    pool.wait_ge(b_used[l], 2 * batch + 2)
                    nc.gpsimd.tensor_tensor(al[:, ds(batch * (KB * H), KB * H)], btmp[:, side, 0:KB * H], ctmp[:, side, 0:KB * H], ALU.add).then_inc(al_step[l], PAIRS_STEP)

                pool.wait_ge(s_keys, 16 * R * l)
                ask_keys(0, 0, kix_count + 1)
                pool.wait_ge(qs_ready, l)
                with pool.Fori(0, batches2) as g:
                    ask_keys(1, 2 * g + 1, kix_count + (2 * g + 2))
                    score(0, g)
                    ask_keys(0, 2 * g + 2, kix_count + (2 * g + 3))
                    score(1, g)
                pool.wait_ge(k_in[l][0], 16 * KB * batches2 + 16 * KB)
                pool.sem_inc(turn, 1)
                kix_count = kix_count + (2 * batches2 + 1)
                for side in range(2):
                    pool.wait_ge(stage_out[l][side], 16 * R * NT // 2)
                pool.wait_ge(rows_go[l], 1)
                gather_rows(l, idxr, ix_count)
                ix_count = ix_count + 2 * groups

        @block.scalar
        def _(act):
            def copy_t(n, out_ap, func=ACT.Copy):
                act.wait_ge(t_ready, n + 1)
                return nc.scalar.activation(out_ap, tbuf(n), func)

            for n in range(NW):
                if n >= 2:
                    act.wait_ge(wt_used, n - 1)
                copy_t(n, wt[n % 2]).then_inc(t_free, 1)
            act.wait_ge(wt_used, NW)
            nc.scalar.activation(wqk[1][:, :, :, :], ps[:, 4, 0:KT * 2 * R * HEADS[1]].rearrange("p (k a q) -> p k a q", k=KT, a=2), ACT.Copy).then_inc(wq_copied, 1)
            for nt in range(NT):
                n = NW + nt
                copy_t(n, hT[:, :, nt * P:(nt + 1) * P], ACT.Relu).then_inc(t_free, 1)
                if nt >= 1:
                    for h in range(2):
                        act.wait_ge(p_ready, 2 * (nt - 1) + h + 1)
                        nc.scalar.activation(hw0[:, nt - 1, h * HALF:(h + 1) * HALF], ps[:, 4 + h, 0:HALF], ACT.Copy).then_inc(hw_ready, 1)
            for h in range(2):
                act.wait_ge(p_ready, 2 * (NT - 1) + h + 1)
                nc.scalar.activation(hw0[:, NT - 1, h * HALF:(h + 1) * HALF], ps[:, 4 + h, 0:HALF], ACT.Copy).then_inc(hw_ready, 1)
            bnd = load_bounds(act)
            act.wait_ge(perm_in, EC)
            for k in range(2 * (SPREAD - 1)):
                nc.scalar.activation(stT[:, ds(bnd[NT] * PAIR + k * P, P)], zero16[:, 0:P], ACT.Copy).then_inc(st_tail, 1)
            with act.Fori(0, bnd[NT]) as i:
                act.wait_ge(st_ready, i + 2)
                nc.scalar.activation(stT[:, ds(i * PAIR, PAIR)], ps[:, ds(i % 2 + 6, 1), 0:P].bitcast(BF16), ACT.Copy).then_inc(st_copied, 1)
            for l in (1, 2):
                H = HEADS[l]
                if l == 1:
                    for nt in range(NT):
                        copy_t(NW + NT + nt, hT[:, :, nt * P:(nt + 1) * P], ACT.Relu).then_inc(t_free, 1)
                for r in range(R):
                    for nt in range(NT):
                        b = nt % 2
                        if r * NT + nt >= 2:
                            act.wait_ge(stage_out[l][b], r * (16 * NT // 2) + 16 * (nt // 2))
                        for h in range(2):
                            act.wait_ge(p_ready, r * (2 * NT) + (2 * NT * (1 + R * (l - 1)) + 2 * nt + h + 1))
                            if H == 4:
                                o = stage[:, b, h * 2 * (HALF // 2 + 1):(h + 1) * 2 * (HALF // 2 + 1)].rearrange("p (a c) -> p a c", a=2)[:, :, 0:HALF // 2]
                                i_ = ps[:, 2 * b + h, 0:HALF].rearrange("p (a c) -> p a c", a=2)
                            else:
                                o = stage[:, b, h * HALF:(h + 1) * HALF]
                                i_ = ps[:, 2 * b + h, 0:HALF]
                            nc.scalar.activation(o, i_, ACT.Copy).then_inc(stage_in[l], 1)
                act.wait_ge(al_ready, l)
                nc.scalar.activation(al[:, 0:T * H], me[:, 0:T * H], ACT.Exp).then_inc(e_ready, 1)
                if l == 1:
                    W = HALF // 2 + 1
                    for j in range(NT):
                        act.wait_ge(rz_ready, j + 1)
                        act.wait_ge(t_ready, NW + 2 * NT + j - 1)
                        for h in range(4):
                            last = nc.scalar.activation(hn[:, j % 2, h * (D // 4):(h + 1) * (D // 4)], ps[:, 2 * (j % 2) + h // 2, (h % 2) * W:(h % 2) * W + D // 4], ACT.Copy, scale=rz[:, h:h + 1])
                        last.then_inc(divided, 1)
                        act.wait_ge(divided, j + 1)
                        act.sem_inc(acc_free[1], 1)
                        act.wait_ge(elu_in, j + 1)
                        if j >= 1:
                            act.wait_ge(hn_ready, 2 * NT + j)
                        nc.scalar.activation(etmp[:, :], hn[:, j % 2, :], ACT.Relu, scale=-1.0).then_inc(elu_neg, 1)
                        act.wait_ge(elu_neg, j + 1)
                        nc.scalar.activation(etmp[:, :], etmp[:, :], ACT.Exp, scale=-1.0).then_inc(elu_exp, 1)
                        if j >= 2:
                            copy_t(NW + 2 * NT + j - 2, hT[:, :, (j - 2) * P:(j - 1) * P]).then_inc(t_free, 1)
                    for j in (NT - 2, NT - 1):
                        copy_t(NW + 2 * NT + j, hT[:, :, j * P:(j + 1) * P]).then_inc(t_free, 1)

        @block.vector
        def _(dve):
            chain = [0]

            def link(ins):
                chain[0] += 1
                ins.then_inc(dve_c, 1)
                dve.wait_ge(dve_c, chain[0])

            V = nc.vector
            V.memset(xs[96:P, NT - 1, :], 0.0).then_inc(xpad, 1)
            dve.wait_ge(pool_c, 7)
            V.tensor_scalar(ident[:, :], iota_f[:, 0:P], iota_p[:, 0:1], None, ALU.is_equal).then_inc(consts, 1)
            V.tensor_scalar(ident16[:, :], iota_f[:, 0:P], iota_p[:, 0:1], None, ALU.is_equal).then_inc(consts, 1)
            V.tensor_scalar(upper[:, :], iota_f[0:EP, 0:P], iota_p[0:EP, 0:1], None, ALU.is_gt).then_inc(consts, 1)

            dve.wait_ge(s_edges, 48)
            link(V.tensor_copy(e_f, e_i))
            link(V.tensor_scalar(t_a, e_f[:, 1, :], 1.0 / P, -(P / 2 - 0.5) / P, ALU.mult, ALU.add))
            link(V.tensor_scalar(t_b, t_a, ROUND, None, ALU.add))
            link(V.tensor_scalar(dtile, t_b, -ROUND, None, ALU.add))
            link(V.scalar_tensor_tensor(dloc, dtile, -float(P), e_f[:, 1, :], ALU.mult, ALU.add))
            V.tensor_scalar(field1, e_f[:, 0, :], 1.0, None, ALU.add)
            link(V.tensor_scalar(t_a, dloc, 1.0, None, ALU.add))
            V.scalar_tensor_tensor(field2, e_f[:, 2, :], float(P), t_a, ALU.mult, ALU.add)
            for j in range(NT):
                last = V.tensor_scalar(bucket[:, j, :], dtile, float(j), None, ALU.is_equal)
            link(last)
            a, b, s = bucket, cumA, 1
            while s < EC:
                V.tensor_copy(b[:, :, 0:s], a[:, :, 0:s])
                link(V.tensor_tensor(b[:, :, s:EC], a[:, :, s:EC], a[:, :, 0:EC - s], ALU.add))
                a, b, s = b, (cumB if b is cumA else cumA), 2 * s
            cum = a
            V.tensor_copy(rowtot, cum[:, :, EC - 1]).then_inc(ranks_in, 1)
            dve.wait_ge(ranks_out, 1)
            link(V.tensor_scalar(cnt[:, :], ps[:, 7, NT:2 * NT], 1.0 / PAIR, (PAIR / 2 - 0.5) / PAIR, ALU.mult, ALU.add))
            link(V.tensor_scalar(tot[:, :], cnt[:, :], ROUND, None, ALU.add))
            V.memset(pstart[:, :, :], 0.0)
            link(V.tensor_scalar(cnt[:, :], tot[:, :], -ROUND, None, ALU.add))
            link(V.tensor_scalar(pstart[:, 0, 1:NT + 1], cnt[:, :], 1.0, None, ALU.max))
            u, s = 0, 1
            while s < NT:
                V.tensor_copy(pstart[:, 1 - u, 1:s + 1], pstart[:, u, 1:s + 1])
                link(V.tensor_tensor(pstart[:, 1 - u, s + 1:NT + 1], pstart[:, u, s + 1:NT + 1], pstart[:, u, 1:NT + 1 - s], ALU.add))
                u, s = 1 - u, 2 * s
            V.tensor_copy(bounds[:, :], pstart[:, u, 0:NT + 1]).then_inc(bounds_ready, 1)
            link(V.scalar_tensor_tensor(base[:, :], pstart[:, u, 0:NT], float(PAIR), ps[:, 7, 0:NT], ALU.mult, ALU.add))
            link(V.tensor_scalar(base[:, :], base[:, :], -1.0, None, ALU.add))
            link(V.tensor_tensor(wpos, cum, base[0:EP, :].unsqueeze(2).to_broadcast([EP, NT, EC]), ALU.add))
            link(V.tensor_tensor(wpos, wpos, bucket, ALU.mult))
            link(V.tensor_reduce(t_a, wpos.rearrange("p j c -> p c j"), AX.X, ALU.add))
            link(V.tensor_scalar(t_b, t_a, 1.0 / P, -(P / 2 - 0.5) / P, ALU.mult, ALU.add))
            link(V.tensor_scalar(t_b, t_b, ROUND, None, ALU.add))
            link(V.tensor_scalar(slot_hi, t_b, -ROUND, None, ALU.add))
            link(V.scalar_tensor_tensor(slot_lo, slot_hi, -float(P), t_a, ALU.mult, ALU.add))
            dve.sem_inc(slots_f, 1)
            def moments(j):
                V.bn_stats(stats[:, 0, :], xs[:, j, 0:HALF])
                link(V.bn_stats(stats[:, 1, :], xs[:, j, HALF:D]))
                link(V.bn_aggr(mv[:, j, :], stats[:, :, :].rearrange("p a c -> p (a c)")))

            for j in range(NT):
                if j % 3 == 0:
                    dve.wait_ge(s_x[j // 3], 16)
                if j == NT - 1:
                    dve.wait_ge(xpad, 1)
                moments(j)
            V.tensor_scalar(vare[:, :], mv[:, :, 1], EPS_LN, None, ALU.add).then_inc(var_ready, 1)
            dve.wait_ge(rstd_ready, 1)

            def edge_groups(first, count):
                with dve.Fori(first, first + count) as g:
                    for b in range(PB):
                        c = ds(g * PB + b, 1)
                        dve.wait_ge(perm_free, g * PB + (b + 1))
                        V.tensor_scalar(oh_lo[:, b, :], iota_h[0:EP, 0:P], slot_lo[:, c], None, ALU.is_equal)
                        V.tensor_scalar(oh_hi[:, b, 0, :], iota_h[0:EP, :], slot_hi[:, c], field1[:, c], ALU.is_equal, ALU.mult)
                        V.tensor_scalar(oh_hi[:, b, 1, :], iota_h[0:EP, :], slot_hi[:, c], field2[:, c], ALU.is_equal, ALU.mult).then_inc(perm_in, 1)

            def prepare(r):
                dve.wait_ge(wprep_in[1], 16 * (2 + r))
                if r == 0:
                    dve.wait_ge(s_qkb, 32)
                for k in range(KT):
                    for a in range(2):
                        n = (r * KT + k) * 2 + a
                        if n >= 2:
                            dve.wait_ge(ttr, n - 1)
                        V.tensor_tensor_reduce(stage[:, a, 0:D], wreg[:, 1, k, :], qkb[:, a, :], 1.0, 0.0, ALU.mult, ALU.add, wqk[2][:, k, a, r:r + 1]).then_inc(ttr, 1)
                dve.wait_ge(ttr, 2 * KT * (r + 1))
                dve.sem_inc(wq2_done, 1)

            sorted_ = len(GROUP_AFTER)
            edge_groups(0, sorted_)
            for j in range(NT):
                if j >= 2:
                    dve.wait_ge(t_ready, NW + j - 1)
                V.tensor_scalar(hn[:, j % 2, :], xs[:, j, :], mv[:, j, 0:1], rstd[:, j:j + 1], ALU.subtract, ALU.mult).then_inc(hn_ready, 1)
                edge_groups(sorted_ + j, 1)
                if j < R:
                    prepare(j)
                if j == 0:
                    dve.wait_ge(s_bias[0], 16)
                for k in BIAS_AT.get(j, ()):
                    V.tensor_tensor(xs[:, k, :], xs[:, k, :], bias[:, :], ALU.add)
            V.memset(stage[:, :, :], 1.0)
            dve.wait_ge(perm_free, EC + PB)
            V.tensor_scalar(deg[:, :], ps[:, 7, 0:NT], 1.0, None, ALU.add).then_inc(deg_ready, 1)
            link(V.tensor_copy(fields[:, :, :], ps[:, 6, 0:2 * T].rearrange("p (f c) -> p f c", f=2)))
            link(V.tensor_scalar(t_s[:, :], fields[:, 0, :], -1.0, 0.0, ALU.add, ALU.max))
            V.tensor_copy(idx0[:, :], t_s[:, :])
            link(V.tensor_scalar(t_r[:, :], fields[:, 1, :], 1.0 / P, -(P / 2 + 0.5) / P, ALU.mult, ALU.add))
            link(V.tensor_scalar(t_r[:, :], t_r[:, :], ROUND, None, ALU.add))
            link(V.tensor_scalar(t_r[:, :], t_r[:, :], -ROUND, 0.0, ALU.add, ALU.max))
            link(V.scalar_tensor_tensor(tl[:, :], t_r[:, :], -float(P), fields[:, 1, :], ALU.mult, ALU.add))
            link(V.tensor_scalar(tl[:, :], tl[:, :], -1.0, None, ALU.add))
            for r in range(R):
                V.tensor_scalar(rmask[:, :, r], t_r[:, :], float(r), None, ALU.is_equal)
            link(V.scalar_tensor_tensor(t_s[:, :], t_r[:, :], float(NP_), t_s[:, :], ALU.mult, ALU.add))
            V.tensor_copy(idxr[:, 0:T], t_s[:, :]).then_inc(slots_ready, 1)
            dve.wait_ge(slots_ready, 1)
            bnd = load_bounds(dve)
            groups = (bnd[NT] + (RING - 1)) // RING
            batches2 = (bnd[NT] + (2 * PAIRS_STEP - 1)) // (2 * PAIRS_STEP)

            dve.wait_ge(dinv_ready, 1)
            link(V.tensor_tensor(dinv2[:, :], dinv[:, :], dinv[:, :], ALU.mult))
            for j in range(NT):
                dve.wait_ge(hw_ready, 2 * j + 2)
                last = V.scalar_tensor_tensor(xs[:, j, :], hw0[:, j, :], dinv2[:, j:j + 1], xs[:, j, :], ALU.mult, ALU.add)
            link(last)

            def finish0(j):
                dve.wait_ge(w_used[0], 2 * bnd[j + 1] + 2 * RING)
                x2 = xs[:, j, :].rearrange("p (a c) -> p a c", a=2)
                bk = 2 * (j % 2)
                link(V.scalar_tensor_tensor(x2, ps[:, bk:bk + 2, 0:HALF], dinv[:, j:j + 1], x2, ALU.mult, ALU.add))
                dve.sem_inc(acc_free[0], 1)
                dve.sem_inc(x1_ready, 1)
                moments(j)

            for j in range(NT):
                with dve.Fori(bnd[j], bnd[j + 1]) as i:
                    for b in range(2):
                        t = 2 * i + b
                        if b == 0:
                            dve.wait_ge(st_ready, i + 1)
                        V.tensor_scalar(s16[:, b, :], iota_h[:, 0:P], tl[:, ds(t, 1)], None, ALU.is_equal).then_inc(o16_in, 1)
                        if b == 0:
                            dve.wait_ge(g_in[0], t + (RING + 3))
                        dve.wait_ge(w_used[0], t + (2 * RING - 1))
                        V.tensor_scalar(zw[:, 0, b, 0, :], iota_f[:, 0:P], tl[:, ds(t, 1)], ring[:, ds((i % RING) * 2 + b, 1), D:D + 1].rearrange("p a c -> p (a c)"), ALU.is_equal, ALU.mult).then_inc(w_in[0], 1)
                if j >= 1:
                    finish0(j - 1)
            finish0(NT - 1)
            V.tensor_scalar(vare[:, :], mv[:, :, 1], EPS_LN, None, ALU.add).then_inc(var_ready, 1)

            def spread_banks(bank, width, stride):
                per = 512 // stride
                for a in range(-(-NPAIR // per)):
                    n = min(per, NPAIR - a * per)
                    c = (bank + a) * 512
                    parts = 1 if H > 1 else 3
                    v = psf[:, c:c + n * stride].rearrange("p (i x) -> p i x", x=stride)[:, :, 0:2 * parts * width]
                    yield 2 * a * per, 2 * n, v

            for l in (1, 2):
                H = HEADS[l]
                if l == 1:
                    dve.wait_ge(rstd_ready, 2)
                    for j in range(NT):
                        dve.wait_ge(t_ready, NW + NT + j - 1)
                        V.tensor_scalar(hn[:, j % 2, :], xs[:, j, :], mv[:, j, 0:1], rstd[:, j:j + 1], ALU.subtract, ALU.mult).then_inc(hn_ready, 1)
                if l == 2:
                    dve.wait_ge(s_keys, 16 * R)
                    for b in range(2):
                        dve.wait_ge(stage_out[1][b], 16 * R * NT // 2)
                    V.memset(stage[:, :, D:D + 1], 1.0)
                dve.wait_ge(qv_done, NT * l)
                for b in range(2):
                    V.tensor_copy(kst[:, :, :, 0:H].rearrange("p r (t b) h -> p b t r h", b=2)[:, b],
                                  ps[:, 5 + 2 * b, 256:256 + NT * R * H].rearrange("p (t a r h) -> p a t r h", a=2, r=R, h=H)[:, 1]).then_inc(kst_ready, 1)
                    last = V.tensor_copy(qv[:, :, 0:R * H].rearrange("p (t b) q -> p b t q", b=2)[:, b],
                                         ps[:, 5 + 2 * b, 256:256 + NT * R * H].rearrange("p (t a q) -> p a t q", a=2, q=R * H)[:, 0])
                link(last)
                for part in range(3):
                    link(V.tensor_copy(q16[:, :, part, 0:R * H], qv[:, :, 0:R * H]))
                    if part < 2:
                        link(V.tensor_tensor(qv[:, :, 0:R * H], qv[:, :, 0:R * H], q16[:, :, part, 0:R * H], ALU.subtract))
                dve.sem_inc(q16_ready, 1)
                dve.wait_ge(g_in[l - 1], 2 * RING * groups + (RING + 1))
                dve.wait_ge(q_spread[l], 1)
                for t0, n, v in spread_banks(BANK_Q, R * H, SQ):
                    for b in range(2):
                        if H == 1:
                            last = V.tensor_reduce(qe[:, 0:T * R].rearrange("p (i b q) -> p b i q", b=2, q=R)[:, b, t0 // 2:(t0 + n) // 2],
                                                   v.rearrange("p i (b c q) -> p b i q c", b=2, c=3)[:, b], AX.X, ALU.add)
                            continue
                        last = V.tensor_tensor(qe[:, 0:T * R * H].rearrange("p (i b r h) -> p b i r h", b=2, r=R, h=H)[:, b, t0 // 2:(t0 + n) // 2],
                                               v.rearrange("p i (b r h) -> p b i r h", b=2, r=R)[:, b],
                                               rmask[:, :, :].rearrange("p (i b) r -> p b i r", b=2)[:, b, t0 // 2:(t0 + n) // 2].unsqueeze(3).to_broadcast([P, n // 2, R, H]), ALU.mult)
                link(last)
                dve.sem_inc(spread_read, 1)
                if H == 1:
                    link(V.tensor_tensor(qe[:, 0:T * R], qe[:, 0:T * R], rmask[:, :, :].rearrange("p t r -> p (t r)"), ALU.mult))
                V.tensor_reduce(qs[:, 0:T * H].rearrange("p (t h) -> p t h", h=H), qe[:, 0:T * R * H].rearrange("p (t r h) -> p t h r", r=R, h=H), AX.X, ALU.add).then_inc(rows_go[l], 1)
                dve.wait_ge(rows_go[l], 1)
                dve.sem_inc(qs_ready, 1)

                if l == 2:
                    dve.wait_ge(s_bias[2], 16)
                    for j in range(NT):
                        last = V.tensor_tensor(xs[:, j, :], xs[:, j, :], bias[:, :], ALU.add)
                    link(last)
                def maxima(j):
                    dve.wait_ge(z_done[l], j + 1)
                    m = mx[:, j, 0:H]
                    V.tensor_reduce(m, psf[:, 4 * 512:4 * 512 + 2 * H * P].rearrange("p (b h e) -> p h b e", b=2, h=H), AX.XY, ALU.max).then_inc(z_read[l], 1)
                    dve.wait_ge(z_read[l], j + 1)
                    link(V.tensor_copy(m16[:, j, 0, 0:H], m))
                    link(V.tensor_tensor(m, m, m16[:, j, 0, 0:H], ALU.subtract))
                    link(V.tensor_copy(m16[:, j, 1, 0:H], m))
                    V.tensor_tensor(m16[:, j, 2, 0:H], m, m16[:, j, 1, 0:H], ALU.subtract).then_inc(m16_ready, 1)

                def mask(i, b):
                    V.tensor_scalar(negm[:, ds(i % 2, 1), b, :].rearrange("p a c -> p (a c)"), iota_f[:, 0:P], tl[:, ds(2 * i + b, 1)], NEG, ALU.not_equal, ALU.mult).then_inc(nm_step[l], 1)

                dve.sem_inc(m_chain[l], 1)
                for b in range(2):
                    V.tensor_scalar(negm[:, 0, b, :], iota_f[:, 0:P], tl[:, b:b + 1], NEG, ALU.not_equal, ALU.mult).then_inc(nm_step[l], 1)
                for j in range(NT):
                    run = zw[:, j % 2, :, 0:H, :]
                    if j >= 2:
                        dve.wait_ge(z_done[l], j - 1)
                    V.memset(run, 2 * NEG).then_inc(m_chain[l], 2)
                    with dve.Fori(bnd[j], bnd[j + 1]) as i:
                        dve.wait_ge(al_step[l], i + 1)
                        dve.wait_ge(nm_step[l], 2 * i + 2)
                        dve.wait_ge(m_chain[l], 2 * i + (2 * j + 3))
                        V.tensor_tensor(scored[:, :, 0:H, :], negm[:, ds(i % 2, 1), :, :].rearrange("p a b c -> p (a b) c").unsqueeze(2).to_broadcast([P, 2, H, P]),
                                        al[:, ds(i * (2 * H), 2 * H)].rearrange("p (b h) -> p b h", b=2).unsqueeze(3).to_broadcast([P, 2, H, P]), ALU.add).then_inc(m_chain[l], 1)
                        for b in range(2):
                            mask(i + 1, b)
                        dve.wait_ge(m_chain[l], 2 * i + (2 * j + 4))
                        V.tensor_tensor(run, run, scored[:, :, 0:H, :], ALU.max).then_inc(m_chain[l], 1)
                    dve.wait_ge(m_chain[l], 2 * bnd[j + 1] + (2 * j + 3))
                    dve.sem_inc(z_in[l], 1)
                    if j >= 1:
                        maxima(j - 1)
                maxima(NT - 1)
                dve.wait_ge(al_step[l], 6 * batches2)
                dve.wait_ge(m_spread[l], 1)
                for t0, n, v in spread_banks(BANK_M, H, SM):
                    if H == 1:
                        for b in range(2):
                            last = V.tensor_reduce(me[:, t0:t0 + n].rearrange("p (i b) -> p b i", b=2)[:, b], v.rearrange("p i (b c) -> p b i c", b=2)[:, b], AX.X, ALU.add)
                        continue
                    last = V.tensor_tensor(me[:, t0 * H:(t0 + n) * H].rearrange("p (i x) -> p i x", x=2 * H), al[:, t0 * H:(t0 + n) * H].rearrange("p (i x) -> p i x", x=2 * H), v, ALU.subtract)
                link(last)
                dve.sem_inc(spread_read, 1)
                if H == 1:
                    link(V.tensor_tensor(me[:, 0:T], al[:, 0:T], me[:, 0:T], ALU.subtract))
                V.tensor_scalar(me[:, 0:T * H], me[:, 0:T * H], 0.0, None, ALU.min).then_inc(al_ready, 1)
                dve.wait_ge(e_ready, l)

                def sums(j):
                    dve.wait_ge(w_used[l], 2 * bnd[j + 1] + 2 * RING)
                    bk = 2 * (j % 2)
                    W = HALF // 2 + 1
                    if l == 1:
                        zs = ps[:, bk:bk + 2, 0:2 * W].rearrange("p a (b c) -> p a b c", b=2)[:, :, :, W - 1]
                        link(V.tensor_scalar(z[:, 0:4].rearrange("p (a b) -> p a b", a=2), zs, EPS_Z, None, ALU.add))
                    else:
                        link(V.tensor_scalar(z[:, 0:1], ps[:, bk + 1, HALF:HALF + 1], EPS_Z, None, ALU.add))
                    link(V.reciprocal(rz[:, 0:H], z[:, 0:H]))

                def add_bias(j):
                    if j == 0:
                        dve.wait_ge(s_bias[1], 16)
                    dve.wait_ge(divided, j + 1)
                    V.tensor_tensor(hn[:, j % 2, :], hn[:, j % 2, :], bias[:, :], ALU.add).then_inc(elu_in, 1)
                    dve.wait_ge(elu_in, j + 1)

                def elu(j):
                    dve.wait_ge(elu_exp, j + 1)
                    V.scalar_tensor_tensor(hn[:, j % 2, :], etmp[:, :], -1.0, hn[:, j % 2, :], ALU.add, ALU.max).then_inc(hn_ready, 1)

                def residual(j):
                    x2 = xs[:, j, :].rearrange("p (a c) -> p a c", a=2)
                    bk = 2 * (j % 2)
                    V.scalar_tensor_tensor(x2, ps[:, bk:bk + 2, 0:HALF], rz[:, 0:1], x2, ALU.mult, ALU.add).then_inc(o_ready, 1)
                    dve.wait_ge(o_ready, j + 1)
                    dve.sem_inc(acc_free[l], 1)

                dve.sem_inc(w_in[l], 1)
                for j in range(NT + 1):
                    if j < NT:
                        with dve.Fori(bnd[j], bnd[j + 1]) as i:
                            dve.wait_ge(g_in[l], 2 * i + (RING + 3))
                            if H > 1:
                                dve.wait_ge(w_in[l], 2 * i + 1)
                                for b in range(2):
                                    V.tensor_scalar(zw[:, 1, b, 0, :], iota_f[:, 0:P], tl[:, ds(2 * i + b, 1)], None, ALU.is_equal).then_inc(onehot_in, 1)
                            for b in range(2):
                                t = 2 * i + b
                                dve.wait_ge(w_used[l], t + (2 * RING - 1))
                                if H > 1:
                                    dve.wait_ge(onehot_in, t + 1)
                                    last = V.tensor_tensor(zw[:, 0, b, :, :], zw[:, 1, b, 0:1, :].to_broadcast([P, H, P]), al[:, ds(t * H, H)].unsqueeze(2).to_broadcast([P, H, P]), ALU.mult)
                                else:
                                    last = V.tensor_scalar(zw[:, 0, b, 0, :], iota_f[:, 0:P], tl[:, ds(t, 1)], al[:, ds(t, 1)], ALU.is_equal, ALU.mult)
                                last.then_inc(w_in[l], 1)
                    if j >= 1:
                        sums(j - 1)
                        if l == 1:
                            dve.sem_inc(rz_ready, 1)
                            if j >= 2:
                                elu(j - 2)
                            add_bias(j - 1)
                        else:
                            residual(j - 1)
                if l == 1:
                    elu(NT - 1)

        @block.tensor
        def _(pe):
            mm = nc.tensor.matmul

            def transposes(n, tile):
                for k in range(KT):
                    last = nc.tensor.transpose(tbuf(n)[:, k * P:(k + 1) * P], tile(k), ident[:, :])
                last.then_inc(t_ready, 1)

            pe.wait_ge(consts, 3)
            pe.wait_ge(s_qk, 32)
            def wq_tile(n):
                r, k = n // KT, n % KT
                H = HEADS[1]
                pe.wait_ge(t_free, n + 1)
                o = ps[:, 4, 0:KT * 2 * R * H].rearrange("p (k a r h) -> p k a r h", k=KT, a=2, r=R)[:, k, :, r, :]
                for f in range(KT):
                    last = mm(o, wt[n % 2][:, f * P:(f + 1) * P], qk1[:, f, :, :], start=(f == 0), stop=(f == KT - 1))
                last.then_inc(wt_used, 1)

            def sort_group(g):
                c = PB * g
                if g == 0:
                    pe.wait_ge(perm_in, 1)
                    mm(ps[:, 6, 0:2 * T], zero16[0:EP, 0:P], zero16[0:EP, 0:2 * T], start=True, stop=False, skip_group_check=True)
                    mm(ps[:, 7, 0:NT], zero16[0:EP, 0:P], zero16[0:EP, 0:NT], start=True, stop=False, skip_group_check=True)
                for b in range(PB):
                    pe.wait_ge(perm_in, c + b + 1)
                    mm(ps[:, 6, 0:2 * T], oh_lo[:, b, :], oh_hi[:, b, :, :].rearrange("p f c -> p (f c)"), start=False, stop=False, skip_group_check=True)
                    pe.wait_ge(tg_in, c + b + 2)
                    mm(ps[:, 7, 0:NT], oh_tg[:, b, :], bucket[:, :, c + b], start=False, stop=False, skip_group_check=True).then_inc(perm_free, 1)

            for n in range(NW):
                r, k = n // KT, n % KT
                if n >= 2:
                    pe.wait_ge(t_free, n - 1)
                if k == 0:
                    pe.wait_ge(wprep_in[r % 2], 16 * (r // 2 + 1))
                transposes(n, lambda f: wreg[:, r % 2, k, f * P:(f + 1) * P])
                if n >= 1:
                    wq_tile(n - 1)
                if n == 1:
                    pe.wait_ge(ranks_in, 1)
                    mm(ps[:, 7, 0:NT], upper[:, :], rowtot, start=True, stop=True)
                    mm(ps[:, 7, NT:2 * NT], ones[:, :], rowtot, start=True, stop=True).then_inc(ranks_out, 1)
                    pe.sem_inc(perm_free, PB)
                if n in GROUP_AFTER:
                    sort_group(GROUP_AFTER.index(n))
            wq_tile(NW - 1)

            pe.wait_ge(s_w0, 16)
            pe.wait_ge(wq_copied, 1)
            for nt in range(NT):
                n = NW + nt
                pe.wait_ge(hn_ready, nt + 1)
                pe.wait_ge(t_free, n - 1)
                for k in range(KT):
                    last = nc.tensor.transpose(tbuf(n)[:, k * P:(k + 1) * P], hn[:, nt % 2, k * P:(k + 1) * P], ident[:, :])
                last.then_inc(t_ready, 1)
                sort_group(len(GROUP_AFTER) + nt)
                pe.wait_ge(t_free, n + 1)
                for h in range(2):
                    if nt >= 1:
                        pe.wait_ge(hw_ready, 2 * (nt - 1) + h + 1)
                    for k in range(KT):
                        last = mm(ps[:, 4 + h, 0:HALF], hT[:, k, nt * P:(nt + 1) * P], w0s[:, k, h * HALF:(h + 1) * HALF], start=(k == 0), stop=(k == KT - 1))
                    last.then_inc(p_ready, 1)

            bnd = load_bounds(pe)

            def open_acc(l, j):
                if j >= 2:
                    pe.wait_ge(acc_free[l], j - 1)
                for a in range(2):
                    mm(ps[:, 2 * (j % 2) + a, 0:HALF + 2], zero16[:, 0:P], zero16[:, 0:HALF + 2], start=True, stop=False, skip_group_check=True)

            def spread_open(bank, stride):
                for a in range(-(-NPAIR * stride // 512)):
                    mm(ps[:, bank + a, :], zero16[:, 0:P], zero16[:, 0:512], start=True, stop=True)

            def spread(j, parts, bank, width, stride):
                apart = 6 * width <= stride
                w = 3 * width if apart else width
                with pe.Fori(bnd[j], bnd[j + 1], SPREAD) as i:
                    for k in range(2 * SPREAD):
                        o = psf[:, ds(i * stride + (bank * 512 + k // 2 * stride + k % 2 * w), w)]
                        onehot = stT[:, ds(i * PAIR + k * P, P)]
                        if apart:
                            mm(o.rearrange("p (c q) -> p c q", c=3), onehot, parts[:, j, :, 0:width], start=True, stop=True)
                            continue
                        for part in range(3):
                            mm(o, onehot, parts[:, j, part, 0:width], start=(part == 0), stop=(part == 2))

            def spread_close(bank, stride, done):
                c = bank * 512 + NPAIR * stride
                mm(psf[:, c:c + 8], zero16[:, 0:P], zero16[:, 0:8], start=True, stop=True).then_inc(done, 1)

            pe.sem_inc(w_used[0], 2 * RING)
            pe.sem_inc(st_copied, 2)
            pe.sem_inc(st_ready, 1)
            for j in range(NT):
                open_acc(0, j)
                with pe.Fori(bnd[j], bnd[j + 1]) as i:
                    for b in range(2):
                        if b == 1:
                            pe.wait_ge(o16_in, 2 * i + 2)
                            pe.wait_ge(st_copied, i + 1)
                            for c in range(2):
                                last = nc.tensor.transpose(ps[:, ds(i % 2 + 6, 1), 0:P].bitcast(BF16).rearrange("p o c -> p (o c)")[:, c * P:(c + 1) * P], s16[:, c, :], ident16[:, :])
                            last.then_inc(st_ready, 1)
                        pe.wait_ge(w_in[0], 2 * i + (b + 1))
                        for a in range(2):
                            last = mm(ps[:, 2 * (j % 2) + a, 0:HALF], zw[:, 0, b, 0, :], ring[:, ds((i % RING) * 2 + b, 1), a * HALF:(a + 1) * HALF].rearrange("p o c -> p (o c)"), start=False, stop=False, skip_group_check=True)
                        last.then_inc(w_used[0], 1)

            def by_node(l, nt):
                n = NW + l * NT + nt
                pe.wait_ge(t_free, n + 1)
                w = 2 * R * HEADS[l]
                c = 256 + nt // 2 * w
                for k in range(KT):
                    last = mm(ps[:, 5 + 2 * (nt % 2), c:c + w], hT[:, k, nt * P:(nt + 1) * P], wqk[l][:, k, :, :].rearrange("p a q -> p (a q)"), start=(k == 0), stop=(k == KT - 1))
                last.then_inc(qv_done, 1)

            def to_features(l, nt):
                n = NW + l * NT + nt
                pe.wait_ge(hn_ready, l * NT + nt + 1)
                pe.wait_ge(t_free, n - 1)
                for k in range(KT):
                    last = nc.tensor.transpose(tbuf(n)[:, k * P:(k + 1) * P], hn[:, nt % 2, k * P:(k + 1) * P], ident[:, :])
                last.then_inc(t_ready, 1)
                if nt >= 1:
                    by_node(l, nt - 1)

            for l in (1, 2):
                H = HEADS[l]
                if l == 1:
                    pe.wait_ge(st_copied, bnd[NT] + 2)
                    for nt in range(NT):
                        to_features(l, nt)
                by_node(l, NT - 1)
                pe.wait_ge(q16_ready, l)
                pe.wait_ge(st_tail, 2 * (SPREAD - 1))
                spread_open(BANK_Q, SQ)
                for j in range(NT):
                    spread(j, q16, BANK_Q, R * H, SQ)
                spread_close(BANK_Q, SQ, q_spread[l])
                pe.wait_ge(spread_read, 2 * l - 1)

                pe.sem_inc(stage_in[l], 4)

                def project(r, nt):
                    for h in range(2):
                        pe.wait_ge(stage_in[l], r * (2 * NT) + (2 * nt + h + 1))
                        for k in range(KT):
                            last = mm(ps[:, 2 * (nt % 2) + h, 0:HALF], hT[:, k, nt * P:(nt + 1) * P], wreg[:, r % 2, k, h * HALF:(h + 1) * HALF], start=(k == 0), stop=(k == KT - 1))
                        last.then_inc(p_ready, 1)

                for r in range(R):
                    pe.wait_ge(s_w[l], r + 1)
                    if r == 1:
                        spread_open(BANK_M, SM)
                    for nt in range(NT):
                        project(r, nt)
                        for n in MAX_AT.get(r * NT + nt, ()):
                            if n < NT:
                                pe.wait_ge(z_in[l], n + 1)
                                if n >= 1:
                                    pe.wait_ge(z_read[l], n)
                                for b in range(2):
                                    for h in range(H):
                                        c = 4 * 512 + (b * H + h) * P
                                        last = nc.tensor.transpose(psf[:, c:c + P], zw[:, n % 2, b, h, :], ident[:, :])
                                last.then_inc(z_done[l], 1)
                            if n >= 2:
                                pe.wait_ge(m16_ready, (l - 1) * NT + n - 1)
                                spread(n - 2, m16, BANK_M, H, SM)
                spread_close(BANK_M, SM, m_spread[l])
                pe.wait_ge(stage_in[l], 4 + 2 * R * NT)
                pe.wait_ge(spread_read, 2 * l)
                pe.sem_inc(w_used[l], 2 * RING)
                for j in range(NT + 1):
                    if j < NT:
                        open_acc(l, j)
                        with pe.Fori(bnd[j], bnd[j + 1]) as i:
                            for b in range(2):
                                pe.wait_ge(w_in[l], 2 * i + (b + 2))
                                row = ring[:, ds((i % RING) * 2 + b, 1), :].rearrange("p o c -> p (o c)")
                                W = HALF // 2 + 1
                                if H == 4:
                                    for h in range(H):
                                        last = mm(ps[:, 2 * (j % 2) + h // 2, (h % 2) * W:(h % 2 + 1) * W], zw[:, 0, b, h, :], row[:, h * W:(h + 1) * W], start=False, stop=False, skip_group_check=True)
                                else:
                                    mm(ps[:, 2 * (j % 2), 0:HALF], zw[:, 0, b, 0, :], row[:, 0:HALF], start=False, stop=False, skip_group_check=True)
                                    last = mm(ps[:, 2 * (j % 2) + 1, 0:HALF + 1], zw[:, 0, b, 0, :], row[:, HALF:D + 1], start=False, stop=False, skip_group_check=True)
                                last.then_inc(w_used[l], 1)
                    if l == 1 and j >= 3:
                        for nt in ([j - 3] if j < NT else [j - 3, j - 2, j - 1]):
                            to_features(2, nt)


_INS = ['x', 'src', 'dst', 'edge_type_3', 'L0_gnn_W', 'L0_gnn_b', 'L1_gnn_W1', 'L1_gnn_q1', 'L1_gnn_k1', 'L1_gnn_b1',
        'L1_gnn_W2', 'L1_gnn_q2', 'L1_gnn_k2', 'L1_gnn_b2']


def kernel(**inputs):
    import numpy as _np
    import concourse.bacc as _bacc
    from concourse import mybir as _mybir
    from concourse.bass_utils import run_bass_kernel_spmd as _run

    nc = _bacc.Bacc("TRN2", target_bir_lowering=False, num_devices=1)
    arrays, args = {}, []
    for name in _INS:
        a = _np.ascontiguousarray(inputs[name])
        arrays[f"in_{name}"] = a
        args.append(nc.dram_tensor(f"in_{name}", a.shape, _mybir.dt.from_np(a.dtype), kind="ExternalInput").ap())
    out = nc.dram_tensor("out_x", (N, D), F32, kind="ExternalOutput").ap()
    gnn_kernel(nc, *args, out)
    r = _run(nc, [arrays], core_ids=[0])
    return r.results[0]["out_x"]
```
